# Optimizing a Trainium2 kernel written in Bass

```python
import numpy as np
import jax
import jax.numpy as jnp

def _softmax(x, axis=-1):
    return jax.nn.softmax(x, axis=axis)

def _gelu(x):
    return jax.nn.gelu(x, approximate=True)

def _silu(x):
    return jax.nn.silu(x)

def _sigmoid(x):
    return jax.nn.sigmoid(x)

def _layernorm(x, axis=-1, eps=1e-05):
    m = jnp.mean(x, axis=axis, keepdims=True)
    v = jnp.var(x, axis=axis, keepdims=True)
    return (x - m) / jnp.sqrt(v + eps)

def _scatter_add(tgt, idx, src, axis=0):
    return tgt.at[idx].add(src)

def _segment_sum(src, seg, n):
    return jax.ops.segment_sum(src, seg, n)
kernel_name = 'mk_recurrent_d1_jaxref_r8_5aaa19'

def setup_inputs(seed: int=0):
    np.random.seed(seed)
    _w = jnp.asarray

    def _L0_attn_setup():
        import jax, jax.numpy as jnp
        import numpy as np
        KEY_DIM = 128
        SCALE = KEY_DIM ** (-0.5)
        key = jax.random.key(seed)
        k1, k2, k3, k4 = jax.random.split(key, 4)
        B, S, E = (4, 256, 128)
        x = jax.random.normal(k1, (B, S, E), dtype=jnp.float32)
        WQ = jax.random.normal(k2, (KEY_DIM, E), dtype=jnp.float32) * E ** (-0.5)
        WK = jax.random.normal(k3, (KEY_DIM, E), dtype=jnp.float32) * E ** (-0.5)
        WV = jax.random.normal(k4, (KEY_DIM, E), dtype=jnp.float32) * E ** (-0.5)
        return {'x': x, 'WQ': WQ, 'WK': WK, 'WV': WV}
    _L0_attn_in = _L0_attn_setup()

    def _L0_ffn_setup():
        import jax, jax.numpy as jnp
        import numpy as np
        EPS = 1e-06
        N_EXPERTS = 8

        def _rms_norm(x, scale, eps=EPS):
            mean_sq = jnp.mean(x.astype(jnp.float32) ** 2, axis=-1, keepdims=True)
            s = scale.astype(jnp.float32) * jax.lax.rsqrt(mean_sq + eps)
            return x * s.astype(x.dtype)

        def _dist2(x, y):
            nx = jnp.sum(x ** 2, axis=-1)[..., :, None]
            ny = jnp.sum(y ** 2, axis=-1)[..., None, :]
            return nx + ny - 2.0 * (x @ y.T)
        key = jax.random.key(seed)
        ks = jax.random.split(key, 5)
        dim, hidden, E = (128, 256, N_EXPERTS)
        x = jax.random.normal(ks[0], (4, 256, dim), dtype=jnp.float32)
        scale = jnp.ones((dim,), dtype=jnp.float32)
        centroids = jax.random.normal(ks[1], (E, dim), dtype=jnp.float32)
        up_w = jax.random.normal(ks[2], (E, dim, hidden * 2), dtype=jnp.float32) * dim ** (-0.5)
        down_w = jax.random.normal(ks[3], (E, hidden, dim), dtype=jnp.float32) * hidden ** (-0.5)
        return {'x': x, 'scale': scale, 'centroids': centroids, 'up_w': up_w, 'down_w': down_w}
    _L0_ffn_in = _L0_ffn_setup()
    _d = {'L0_attn_x': _L0_attn_in['x'], 'L0_attn_WQ': _L0_attn_in['WQ'], 'L0_attn_WK': _L0_attn_in['WK'], 'L0_attn_WV': _L0_attn_in['WV'], 'L0_ffn_scale': _L0_ffn_in['scale'], 'L0_ffn_centroids': _L0_ffn_in['centroids'], 'L0_ffn_up_w': _L0_ffn_in['up_w'], 'L0_ffn_down_w': _L0_ffn_in['down_w']}
    _x0 = _d['L0_attn_x']
    _d['L0_attn_x'] = jax.random.normal(jax.random.fold_in(jax.random.key(seed), 1), (4, 512, 128), dtype=_x0.dtype)
    del _x0
    return _d

def reference(L0_attn_x, L0_attn_WQ, L0_attn_WK, L0_attn_WV, L0_ffn_scale, L0_ffn_centroids, L0_ffn_up_w, L0_ffn_down_w):

    def _L0_attn_ref(x, WQ, WK, WV):
        import jax, jax.numpy as jnp
        import numpy as np
        KEY_DIM = 128
        SCALE = KEY_DIM ** (-0.5)
        q = jnp.einsum('bse,ke->bsk', x, WQ)
        k = jnp.einsum('bse,ke->bsk', x, WK)
        v = jnp.einsum('bse,ve->bsv', x, WV)
        scores = jnp.einsum('bsk,btk->bst', q, k) * SCALE
        masked = jnp.where(jnp.tril(scores) == 0, -jnp.inf, scores)
        attn = jax.nn.softmax(masked, axis=-1)
        return jnp.einsum('bst,btv->bsv', attn, v)

    def _L0_ffn_ref(x, scale, centroids, up_w, down_w):
        import jax, jax.numpy as jnp
        import numpy as np
        EPS = 1e-06
        N_EXPERTS = 8

        def _rms_norm(x, scale, eps=EPS):
            mean_sq = jnp.mean(x.astype(jnp.float32) ** 2, axis=-1, keepdims=True)
            s = scale.astype(jnp.float32) * jax.lax.rsqrt(mean_sq + eps)
            return x * s.astype(x.dtype)

        def _dist2(x, y):
            nx = jnp.sum(x ** 2, axis=-1)[..., :, None]
            ny = jnp.sum(y ** 2, axis=-1)[..., None, :]
            return nx + ny - 2.0 * (x @ y.T)
        skip = x
        xn = _rms_norm(x, scale)
        ids = jnp.argmin(_dist2(xn, centroids), axis=-1)
        out = jnp.zeros_like(x)
        for e in range(N_EXPERTS):
            h = jnp.einsum('bsd,dh->bsh', xn, up_w[e])
            a, g = jnp.split(h, 2, axis=-1)
            y = jnp.einsum('bsh,hd->bsd', a * jax.nn.silu(g), down_w[e])
            out = jnp.where((ids == e)[..., None], y, out)
        return out + skip
    x = L0_attn_x
    xn = _layernorm(x, axis=-1)
    s = _L0_attn_ref(xn, L0_attn_WQ, L0_attn_WK, L0_attn_WV)
    g = _silu(_L0_ffn_ref(xn, L0_ffn_scale, L0_ffn_centroids, L0_ffn_up_w, L0_ffn_down_w))
    x = x + s * g
    return x

_drawn_inputs = setup_inputs


def setup_inputs(seed=0):
    import zlib

    import numpy as np

    out = dict(_drawn_inputs(seed))
    spreads = {'L0_ffn_scale': (1.0, 0.2)}
    factors = {}
    for name, (base, spread) in spreads.items():
        noise = np.random.default_rng([zlib.crc32(name.encode()), seed]).standard_normal(out[name].shape)
        drawn = base * np.exp(spread * noise) if base else spread * noise
        out[name] = jnp.asarray(drawn.astype(out[name].dtype))
    for name, factor in factors.items():
        out[name] = (out[name] * factor).astype(out[name].dtype)
    return out
```

```python
import concourse.bass as bass
from concourse import mybir
from contextlib import ExitStack

F32 = mybir.dt.float32
BF16 = mybir.dt.bfloat16
I32 = mybir.dt.int32
ALU = mybir.AluOpType
ACT = mybir.ActivationFunctionType
AX = mybir.AxisListType

P = 128
MASKED = -1e30
MAX_FLOOR = -1e29
LN_EPS = 1e-5
RMS_EPS = 1e-6


def build(nc, x_in, wq_in, wk_in, wv_in, scale_in, cent_in, up_in, down_in, out, xf_dram, gate_dram):
    B, S, D = x_in.shape
    E = cent_in.shape[0]
    H = down_in.shape[1]
    H2 = 2 * H
    T = B * S
    NT = T // P
    TB = S // P
    HC = H // P
    SLOT_TILES = NT + E - 1
    SCALE = float(D) ** -0.5
    HALF = NT // 2
    OUT_OF_RANGE = 2 * T
    RING = 4
    assert D == P and S == 512 and H2 == 512 and TB == 4

    x_rows = x_in.rearrange("b s d -> (b s) d")
    x_tiles = x_rows.rearrange("(i p) d -> p i d", p=P)
    out_tiles = out.rearrange("b s d -> (b s) d").rearrange("(i p) d -> p i d", p=P)
    xf_tiles = xf_dram.rearrange("(i p) d -> p i d", p=P)
    gate_tiles = gate_dram.rearrange("(i p) d -> p i d", p=P)

    with ExitStack() as ctx:
        def sb(name, shape, dt=F32):
            return ctx.enter_context(nc.sbuf_tensor(name, shape, dt))

        def sem(name):
            return ctx.enter_context(nc.semaphore(name))

        bank = [ctx.enter_context(nc.psum_tensor(f"bank{n}", [P, 512], F32)) for n in range(8)]

        x = sb("x", [P, NT, D])
        wq, wk, wv = sb("wq", [P, D]), sb("wk", [P, D]), sb("wv", [P, D])
        cent = sb("cent", [E, D])
        scale = sb("scale", [P, 1])
        up = sb("up", [P, E * H2])
        down = sb("down", [P, E * HC * D])
        ident = sb("ident", [P, P])
        ident_bf = sb("ident_bf", [P, P], BF16)
        causal = sb("causal", [P, P], BF16)
        before = sb("before", [P, P], BF16)
        ones_bf = sb("ones_bf", [P, P], BF16)
        ones = sb("ones", [P, P])
        lane = sb("lane", [P, P])
        slot_tile_no = sb("slot_tile_no", [P, SLOT_TILES])
        token_no = sb("token_no", [P, NT])
        expert_no = sb("expert_no", [P, E, NT])
        tile_floor = sb("tile_floor", [P, E, NT])
        carry_on = sb("carry_on", [P, E, NT])
        bn = sb("bn", [P, NT, 6])
        st = {n: sb("st_" + n, [P, NT]) for n in
              ("sum", "dif", "m2", "mean", "dsq", "ssq", "var", "inv", "xf_mul", "rms2")}
        rad = sb("rad", [P, 2, NT])
        root = sb("root", [P, 2, NT])
        rroot = sb("rroot", [P, 2, NT])
        xn = sb("xn", [P, NT, D])
        xf = sb("xf", [P, NT, D])
        xnT = sb("xnT", [P, T])
        xnT_sq = sb("xnT_sq", [P, T])
        qk = sb("qk", [P, D])
        wvT = sb("wvT", [P, D])
        zT = sb("zT", [P, T])
        pen = sb("pen", [P, 2, S])
        prob = sb("prob", [P, 3, S])
        row_max = sb("row_max", [P, NT])
        neg_max = sb("neg_max", [P, NT])
        row_sum = sb("row_sum", [P, NT])
        row_inv = sb("row_inv", [P, NT])
        probT = sb("probT", [P, 2, TB, S])
        mixT = sb("mixT", [P, 2, S])
        attn = sb("attn", [P, NT, D])
        centT_scaled = sb("centT_scaled", [P, E])
        centT_sq = sb("centT_sq", [P, E])
        scale_sq = sb("scale_sq", [P, 1])
        nx = sb("nx", [P, NT])
        rt = {n: sb("rt_" + n, [P, E, NT]) for n in
              ("dot", "norms", "dist", "eq", "eqw", "cum", "excl", "gt", "base", "full", "pick")}
        dmin, amin = sb("dmin", [P, NT]), sb("amin", [P, NT])
        onehot = sb("onehot", [P, E, NT], BF16)
        tiles_of, tiles_end, tiles_start = (sb(n, [P, E]) for n in ("tiles_of", "tiles_end", "tiles_start"))
        slot = sb("slot", [P, NT], I32)
        slot_lane, slot_tile = sb("slot_lane", [P, NT], I32), sb("slot_tile", [P, NT], I32)
        hot_lane = sb("hot_lane", [P, NT, P])
        hot_tile = sb("hot_tile", [P, NT, SLOT_TILES])
        hot_val = sb("hot_val", [P, NT, 2, SLOT_TILES])
        token_of = sb("token_of", [P, SLOT_TILES])
        inv_rms_of = sb("inv_rms_of", [P, SLOT_TILES])
        skip_add = sb("skip_add", [P, SLOT_TILES])
        gather_idx = sb("gather_idx", [P, SLOT_TILES], I32)
        scatter_idx = sb("scatter_idx", [P, SLOT_TILES], I32)
        ended = sb("ended", [P, SLOT_TILES, E])
        ended_sum = sb("ended_sum", [P, SLOT_TILES])
        expert_of = sb("expert_of", [P, SLOT_TILES], I32)
        rows = sb("rows", [P, RING, D])
        rowsT = sb("rowsT", [P, 2, P])
        silu_g = sb("silu_g", [P, 2, H])
        hid = sb("hid", [P, 2, H])
        hidT = sb("hidT", [P, 2, HC, P])
        skip = sb("skip", [P, RING, D])
        gate_in = sb("gate_in", [P, 2, D])
        gate = sb("gate", [P, RING, D])
        gate_tok = sb("gate_tok", [P, NT, D])
        fin = sb("fin", [P, NT, D])

        x_loaded = [sem(f"x_loaded{b}") for b in range(B)]
        qk_loaded, v_loaded, small_loaded = sem("qk_loaded"), sem("v_loaded"), sem("small_loaded")
        up_loaded, down_loaded = sem("up_loaded"), sem("down_loaded")
        zeroed, ident_made, consts_made = sem("zeroed"), sem("ident_made"), sem("consts_made")
        stat_step, rad_ready, root_ready, stats_ready = (
            sem(n) for n in ("stat_step", "rad_ready", "root_ready", "stats_ready"))
        xn_ready, xf_ready = sem("xn_ready"), sem("xf_ready")
        xf_stored = [sem(f"xf_stored{b}") for b in range(B)]
        weights_psum, weights_ready = sem("weights_psum"), sem("weights_ready")
        norms_psum = sem("norms_psum")
        xnT_psum, xnT_ready, sq_ready = sem("xnT_psum"), sem("xnT_ready"), sem("sq_ready")
        zT_psum, zT_ready = sem("zT_psum"), sem("zT_ready")
        dist_psum = sem("dist_psum")
        score_psum, pen_ready, masked_ready, max_ready, prob_ready = (
            sem(n) for n in ("score_psum", "pen_ready", "masked_ready", "max_ready", "prob_ready"))
        probT_psum, probT_ready = sem("probT_psum"), sem("probT_ready")
        mixT_psum, mixT_ready = sem("mixT_psum"), sem("mixT_ready")
        attn_psum, attn_ready, row_inv_ready = sem("attn_psum"), sem("attn_ready"), sem("row_inv_ready")
        route_step, onehot_ready, rank_psum = sem("route_step"), sem("onehot_ready"), sem("rank_psum")
        hot_ready, slots_psum, idx_ready, expert_ready = (
            sem(n) for n in ("hot_ready", "slots_psum", "idx_ready", "expert_ready"))
        gathered = [sem(f"gathered{k}") for k in range(RING)]
        scattered = [sem(f"scattered{k}") for k in range(RING)]
        rowsT_psum, rowsT_ready, up_psum, silu_ready, hid_ready = (
            sem(n) for n in ("rowsT_psum", "rowsT_ready", "up_psum", "silu_ready", "hid_ready"))
        hidT_psum, hidT_ready, down_psum, skip_ready, gate_in_ready, gate_ready = (
            sem(n) for n in ("hidT_psum", "hidT_ready", "down_psum", "skip_ready", "gate_in_ready", "gate_ready"))
        gates_loaded = [sem(f"gates_loaded{b}") for b in range(B)]
        prod_ready, fin_ready, stored = sem("prod_ready"), sem("fin_ready"), sem("stored")

        xnT_bank = bank[0:4]
        zT_bank = [bank[4], bank[5], bank[6], bank[4]]
        route_bank = bank[7]
        dist_ps = route_bank[:, 0:NT * 16].rearrange("p (i c) -> p i c", c=16)
        norm_ps = route_bank[:, 256:256 + E]
        rank_ps = route_bank[:, 0:E * NT]
        count_ps = route_bank[:, E * NT:2 * E * NT]
        slots_ps = route_bank[:, 256:256 + 2 * SLOT_TILES]
        SCORE_BANKS, PROBT_BANKS = 3, 2
        score_bank = bank[0:3]
        probT_bank = bank[3:5]
        mixT_bank, attn_bank = bank[5], bank[6]
        up_bank = bank[0:2]
        hidT_bank = bank[2:4]
        rowsT_bank = [bank[4], bank[7]]
        down_bank = bank[5:7]

        def width(q):
            return (q + 1) * P

        LAST = SLOT_TILES - 1
        LOOPED = (LAST - 3) // RING * RING

        def expert_steps(eng, step):
            for n in range(-1, 3):
                step(n, 0)
            with eng.Fori(0, LOOPED, RING) as shift:
                for n in range(3, 3 + RING):
                    step(n, shift)
            for n in range(3 + LOOPED, LAST + 4):
                step(n, 0)

        def exists(t):
            return 0 <= t <= LAST

        def ring_count(t, shift):
            return 16 * (t // RING + 1) + shift * (16 // RING)

        block = ctx.enter_context(nc.Block())

        @block.sync
        def _(sp):
            for b in range(B):
                sp.dma_start(x[:, b * TB:(b + 1) * TB, :], x_tiles[:, b * TB:(b + 1) * TB, :]
                             ).then_inc(x_loaded[b], 16)
            sp.dma_start(up[:, :].rearrange("p (e n) -> p e n", e=E), up_in.rearrange("e d h -> d e h")
                         ).then_inc(up_loaded, 16)
            sp.dma_start(down[:, :].rearrange("p (e c n) -> p e c n", e=E, c=HC),
                         down_in.rearrange("e (c p) d -> p e c d", p=P)).then_inc(down_loaded, 16)
            for b in range(B):
                sp.wait_ge(xf_ready, (b + 1) * TB)
                sp.dma_start(xf_tiles[:, b * TB:(b + 1) * TB, :], xf[:, b * TB:(b + 1) * TB, :]
                             ).then_inc(xf_stored[b], 16)
            for k in range(RING):
                sp.wait_ge(scattered[k], 16 * len(range(k, SLOT_TILES, RING)))
            for b in range(B):
                sp.dma_start(gate_tok[:, b * TB:(b + 1) * TB, :], gate_tiles[:, b * TB:(b + 1) * TB, :]
                             ).then_inc(gates_loaded[b], 16)
            for b in range(B):
                sp.wait_ge(fin_ready, b + 1)
                sp.dma_start(out_tiles[:, b * TB:(b + 1) * TB, :], fin[:, b * TB:(b + 1) * TB, :]
                             ).then_inc(stored, 16)
            sp.wait_ge(stored, 16 * B)

        @block.gpsimd
        def _(pool):
            g = nc.gpsimd
            g.memset(ident[:, :], 0.0).then_inc(zeroed, 1)
            g.memset(ident_bf[:, :], 0.0).then_inc(zeroed, 1)
            g.memset(causal[:, :], 0.0).then_inc(zeroed, 1)
            g.memset(before[:, :], 1.0).then_inc(zeroed, 1)
            g.memset(ones[:, :], 1.0).then_inc(zeroed, 1)
            pool.wait_ge(zeroed, 5)
            g.affine_select(out=ident[:, :], in_=ident[:, :], compare_op=ALU.not_equal, fill=1.0, base=0,
                            pattern=[[-1, P]], channel_multiplier=1).then_inc(ident_made, 1)
            g.affine_select(out=ident_bf[:, :], in_=ident_bf[:, :], compare_op=ALU.not_equal, fill=1.0,
                            base=0, pattern=[[-1, P]], channel_multiplier=1).then_inc(ident_made, 1)
            g.affine_select(out=causal[:, :], in_=causal[:, :], compare_op=ALU.is_ge, fill=MASKED, base=0,
                            pattern=[[-1, P]], channel_multiplier=1).then_inc(ident_made, 1)
            g.affine_select(out=before[:, :], in_=before[:, :], compare_op=ALU.is_ge, fill=0.0, base=-1,
                            pattern=[[1, P]], channel_multiplier=-1).then_inc(consts_made, 1)
            g.memset(ones_bf[:, :], 1.0).then_inc(consts_made, 1)
            g.memset(carry_on[:, :, 1:NT], 1.0).then_inc(consts_made, 1)
            g.memset(carry_on[:, :, 0:1], 0.0).then_inc(consts_made, 1)

            def count(dst, pattern, base, lanes):
                g.iota(dst, pattern=pattern, base=base, channel_multiplier=lanes,
                       allow_small_or_imprecise_dtypes=True).then_inc(consts_made, 1)

            count(expert_no[:, :, :], [[1, E], [0, NT]], -E, 0)
            count(tile_floor[:, :, :], [[0, E], [P, NT]], 0, 0)
            count(lane[:, :], [[1, P]], 0, 0)
            count(slot_tile_no[:, :], [[1, SLOT_TILES]], 0, 0)
            count(token_no[:, :], [[P, NT]], 1, 1)
            for b in range(B):
                if b % 2 == 0:
                    pool.wait_ge(stats_ready, b // 2 + 1)
                for i in range(b * TB, (b + 1) * TB):
                    g.tensor_scalar(xf[:, i, :], x[:, i, :], st["mean"][:, i:i + 1], st["xf_mul"][:, i:i + 1],
                                    ALU.subtract, ALU.mult).then_inc(xf_ready, 1)
            for b in range(B):
                pool.wait_ge(xf_stored[b], 16)

            def gather(t):
                k = t % RING
                if t >= RING:
                    pool.wait_ge(rowsT_psum, t - RING + 1)
                    pool.wait_ge(skip_ready, t - RING + 1)
                g.indirect_dma_start(rows[:, k, :], None, xf_dram,
                                     bass.IndirectOffsetOnAxis(gather_idx[:, t:t + 1], 0)
                                     ).then_inc(gathered[k], 16)

            def scatter(t):
                pool.wait_ge(gate_ready, t + 1)
                g.indirect_dma_start(gate_dram, bass.IndirectOffsetOnAxis(scatter_idx[:, t:t + 1], 0),
                                     gate[:, t % RING, :], None, bounds_check=T - 1, oob_is_err=False
                                     ).then_inc(scattered[t % RING], 16)

            pool.wait_ge(idx_ready, 2)
            for t in range(SLOT_TILES + RING):
                if t < SLOT_TILES:
                    gather(t)
                if t >= RING:
                    scatter(t - RING)

        @block.scalar
        def _(act):
            a = nc.scalar
            act.dma_start(wq[:, :], wq_in).then_inc(qk_loaded, 16)
            act.dma_start(wk[:, :], wk_in).then_inc(qk_loaded, 16)
            act.dma_start(wv[:, :], wv_in).then_inc(v_loaded, 16)
            act.dma_start(cent[:, :], cent_in).then_inc(small_loaded, 16)
            act.dma_start(scale[:, :], scale_in.rearrange("(p a) -> p a", a=1)).then_inc(small_loaded, 16)
            def copy_z(b):
                act.wait_ge(zT_psum, b + 1)
                a.activation(zT[:, b * S:(b + 1) * S], zT_bank[b][:, :], ACT.Copy).then_inc(zT_ready, 1)

            def copy_probT(n):
                b, q = divmod(n, TB)
                act.wait_ge(probT_psum, n + 1)
                if q == 0 and b >= 2:
                    act.wait_ge(mixT_psum, b - 1)
                a.activation(probT[:, b % 2, 0:q + 1, q * P:(q + 1) * P],
                                     probT_bank[n % 2][:, 0:width(q)].rearrange("p (j c) -> p j c", c=P),
                                     ACT.Copy).then_inc(probT_ready, 1)

            def copy_mix(b):
                act.wait_ge(mixT_psum, b + 1)
                if b >= 2:
                    act.wait_ge(attn_psum, b - 1)
                a.activation(mixT[:, b % 2, :], mixT_bank[:, :], ACT.Copy).then_inc(mixT_ready, 1)

            act.wait_ge(weights_psum, 1)
            a.activation(qk[:, :], bank[4][:, 0:D], ACT.Copy).then_inc(weights_ready, 1)
            act.wait_ge(weights_psum, 2)
            a.activation(wvT[:, :], bank[5][:, 0:D], ACT.Copy).then_inc(weights_ready, 1)
            act.wait_ge(weights_psum, 3)
            act.wait_ge(small_loaded, 32)
            a.activation(centT_sq[:, :], bank[6][:, 0:E], ACT.Square).then_inc(weights_ready, 1)
            a.activation(centT_scaled[:, :], bank[6][:, 0:E], ACT.Identity, bias=0.0,
                         scale=scale[:, 0:1]).then_inc(weights_ready, 1)
            a.activation(scale_sq[:, :], scale[:, :], ACT.Square).then_inc(weights_ready, 1)
            for h in range(2):
                act.wait_ge(rad_ready, h + 1)
                sl = slice(h * HALF, (h + 1) * HALF)
                a.activation(root[:, :, sl], rad[:, :, sl], ACT.Sqrt).then_inc(root_ready, 1)
            for b in range(B):
                cols = slice(b * S, (b + 1) * S)
                act.wait_ge(xnT_psum, b + 1)
                a.activation(xnT[:, cols], xnT_bank[b][:, :], ACT.Copy).then_inc(xnT_ready, 1)
                a.activation(xnT_sq[:, cols], xnT_bank[b][:, :], ACT.Square).then_inc(sq_ready, 1)
                if b >= 1:
                    copy_z(b - 1)
            copy_z(B - 1)
            for n in range(NT + 3):
                if n < NT:
                    w = width(n % TB)
                    act.wait_ge(max_ready, n + 1)
                    a.activation(prob[:, n % 3, 0:w], prob[:, n % 3, 0:w], ACT.Exp, bias=neg_max[:, n:n + 1],
                                 scale=SCALE, accum_out=row_sum[:, n:n + 1]).then_inc(prob_ready, 1)
                if 0 <= n - 2 < NT:
                    copy_probT(n - 2)
                if n >= 6 and (n - 6) % TB == 0:
                    copy_mix((n - 6) // TB)

            def step(n, shift):
                t = n - 3
                if exists(t):
                    act.wait_ge(gate_in_ready, t + 1 + shift)
                    if t >= RING or not isinstance(shift, int):
                        act.wait_ge(scattered[t % RING], ring_count(t - RING, shift))
                    a.activation(gate[:, t % RING, :], gate_in[:, t % 2, :], ACT.Silu).then_inc(gate_ready, 1)
                t = n
                if exists(t):
                    act.wait_ge(up_psum, t + 1 + shift)
                    if t >= 2:
                        act.wait_ge(hid_ready, t - 1 + shift)
                    a.activation(silu_g[:, t % 2, :], up_bank[t % 2][:, H:H2], ACT.Silu).then_inc(silu_ready, 1)
                t = n - 1
                if exists(t):
                    act.wait_ge(hidT_psum, t + 1 + shift)
                    if t >= 2:
                        act.wait_ge(down_psum, t - 1 + shift)
                    a.activation(hidT[:, t % 2, :, :], hidT_bank[t % 2][:, 0:H].rearrange("p (c j) -> p c j", c=HC),
                                 ACT.Copy).then_inc(hidT_ready, 1)

            expert_steps(act, step)

        @block.vector
        def _(dve):
            v = nc.vector
            steps = [0]

            def link(ins):
                steps[0] += 1
                ins.then_inc(stat_step, 1)
                dve.wait_ge(stat_step, steps[0])

            def moments(b):
                dve.wait_ge(x_loaded[b], 16)
                for i in range(b * TB, (b + 1) * TB):
                    last = v.bn_stats(bn[:, i, :], x[:, i, :])
                link(last)

            def statistics(h):
                sl = slice(h * HALF, (h + 1) * HALF)
                s_ = {n: t[:, sl] for n, t in st.items()}
                mean_e, m2_e, mean_o, m2_o = (bn[:, sl, c] for c in (1, 2, 4, 5))
                v.tensor_tensor(s_["sum"], mean_e, mean_o, ALU.add)
                v.tensor_tensor(s_["m2"], m2_e, m2_o, ALU.add)
                link(v.tensor_tensor(s_["dif"], mean_e, mean_o, ALU.subtract))
                link(v.tensor_tensor(s_["dsq"], s_["dif"], s_["dif"], ALU.mult))
                link(v.scalar_tensor_tensor(out=s_["ssq"], in0=s_["dsq"], scalar=D / 4, in1=s_["m2"],
                                            op0=ALU.mult, op1=ALU.add))
                v.tensor_scalar(s_["var"], s_["ssq"], 1.0 / D, None, ALU.mult)
                link(v.tensor_scalar(rad[:, 0, sl], s_["ssq"], 1.0 / D, LN_EPS, ALU.mult, ALU.add))
                link(v.reciprocal(s_["inv"], rad[:, 0, sl]))
                link(v.tensor_tensor(s_["dif"], s_["var"], s_["inv"], ALU.mult))
                v.tensor_scalar(rad[:, 1, sl], s_["dif"], RMS_EPS, None, ALU.add).then_inc(rad_ready, 1)
                link(v.tensor_scalar(s_["mean"], s_["sum"], 0.5, None, ALU.mult))

            def normalise(h):
                sl = slice(h * HALF, (h + 1) * HALF)
                dve.wait_ge(root_ready, h + 1)
                link(v.reciprocal(rroot[:, :, sl], root[:, :, sl]))
                v.tensor_tensor(st["rms2"][:, sl], rroot[:, 1, sl], rroot[:, 1, sl], ALU.mult)
                v.tensor_tensor(st["xf_mul"][:, sl], rroot[:, 0, sl], rroot[:, 1, sl], ALU.mult
                                ).then_inc(stats_ready, 1)
                for i in range(h * HALF, (h + 1) * HALF):
                    v.tensor_scalar(xn[:, i, :], x[:, i, :], st["mean"][:, i:i + 1], rroot[:, 0, i:i + 1],
                                    ALU.subtract, ALU.mult).then_inc(xn_ready, 1)

            moments(0)
            moments(1)
            statistics(0)
            moments(2)
            moments(3)
            normalise(0)
            statistics(1)
            normalise(1)

            def over_tiles(ap):
                return ap.unsqueeze(2).broadcast_to([P, E, NT])

            def over_experts(ap):
                return ap.unsqueeze(1).broadcast_to([P, E, NT])

            def choose_experts():
                dve.wait_ge(consts_made, 9)
                dve.wait_ge(dist_psum, 1)
                link(v.tensor_tensor(nx[:, :], dist_ps[:, :, E], st["rms2"][:, :], ALU.mult))
                link(v.tensor_tensor(rt["norms"][:, :, :], over_experts(nx[:, :]), over_tiles(norm_ps), ALU.add))
                link(v.scalar_tensor_tensor(out=rt["dot"][:, :, :],
                                            in0=dist_ps[:, :, 0:E].rearrange("p i e -> p e i"), scalar=-2.0,
                                            in1=over_experts(rroot[:, 1, :]), op0=ALU.mult, op1=ALU.mult))
                link(v.tensor_tensor(rt["dist"][:, :, :], rt["norms"][:, :, :], rt["dot"][:, :, :], ALU.add))
                link(v.tensor_reduce(dmin[:, :], rt["dist"][:, :, :].rearrange("p e i -> p i e"), AX.X, ALU.min))
                link(v.tensor_tensor(rt["eq"][:, :, :], rt["dist"][:, :, :], over_experts(dmin[:, :]), ALU.is_equal))
                link(v.tensor_tensor(rt["eqw"][:, :, :], rt["eq"][:, :, :], expert_no[:, :, :], ALU.mult))
                link(v.tensor_reduce(amin[:, :], rt["eqw"][:, :, :].rearrange("p e i -> p i e"), AX.X, ALU.min))
                v.tensor_tensor(onehot[:, :, :], expert_no[:, :, :], over_experts(amin[:, :]), ALU.is_equal
                                ).then_inc(onehot_ready, 1)

            def place_tokens():
                flat = "p e i -> p (e i)"
                dve.wait_ge(rank_psum, 1)
                link(v.tensor_tensor_scan(rt["cum"][:, :, :].rearrange(flat), carry_on[:, :, :].rearrange(flat),
                                          count_ps, 0.0, ALU.mult, ALU.add))
                v.tensor_tensor(rt["excl"][:, :, :].rearrange(flat), rt["cum"][:, :, :].rearrange(flat),
                                count_ps, ALU.subtract)
                link(v.tensor_tensor(rt["gt"][:, :, :], over_tiles(rt["cum"][:, :, NT - 1]), tile_floor[:, :, :],
                                     ALU.is_gt))
                link(v.tensor_reduce(tiles_of[:, :], rt["gt"][:, :, :], AX.X, ALU.add))
                link(v.tensor_tensor_scan(tiles_end[:, :], ones[:, 0:E], tiles_of[:, :], 0.0, ALU.mult, ALU.add))
                link(v.tensor_tensor(tiles_start[:, :], tiles_end[:, :], tiles_of[:, :], ALU.subtract))
                link(v.scalar_tensor_tensor(out=rt["base"][:, :, :], in0=over_tiles(tiles_start[:, :]),
                                            scalar=float(P), in1=rt["excl"][:, :, :], op0=ALU.mult, op1=ALU.add))
                link(v.tensor_tensor(rt["full"][:, :, :].rearrange(flat), rt["base"][:, :, :].rearrange(flat),
                                     rank_ps, ALU.add))
                link(v.tensor_tensor(rt["pick"][:, :, :], rt["full"][:, :, :], onehot[:, :, :], ALU.mult))
                with nc.allow_low_precision(reason="the slots are whole numbers below 2^24"):
                    link(v.tensor_reduce(slot[:, :], rt["pick"][:, :, :].rearrange("p e i -> p i e"), AX.X, ALU.add))
                v.tensor_scalar(slot_lane[:, :], slot[:, :], P - 1, None, ALU.bitwise_and)
                link(v.tensor_scalar(slot_tile[:, :], slot[:, :], 7, None, ALU.logical_shift_right))
                v.tensor_tensor(hot_lane[:, :, :], slot_lane[:, :].unsqueeze(2).broadcast_to([P, NT, P]),
                                lane[:, :].unsqueeze(1).broadcast_to([P, NT, P]), ALU.is_equal)
                shape = [P, NT, SLOT_TILES]
                link(v.tensor_tensor(hot_tile[:, :, :], slot_tile[:, :].unsqueeze(2).broadcast_to(shape),
                                     slot_tile_no[:, :].unsqueeze(1).broadcast_to(shape), ALU.is_equal))
                v.tensor_tensor(hot_val[:, :, 0, :], hot_tile[:, :, :],
                                token_no[:, :].unsqueeze(2).broadcast_to(shape), ALU.mult)
                v.tensor_tensor(hot_val[:, :, 1, :], hot_tile[:, :, :],
                                root[:, 1, :].unsqueeze(2).broadcast_to(shape), ALU.mult).then_inc(hot_ready, 1)
                shape = [P, SLOT_TILES, E]
                link(v.tensor_tensor(ended[:, :, :], tiles_end[:, :].unsqueeze(1).broadcast_to(shape),
                                     slot_tile_no[:, :].unsqueeze(2).broadcast_to(shape), ALU.is_le))
                link(v.tensor_reduce(ended_sum[:, :], ended[:, :, :], AX.X, ALU.add))
                v.tensor_scalar(expert_of[:, :], ended_sum[:, :], float(E - 1), None, ALU.min
                                ).then_inc(expert_ready, 1)

            def index_slots():
                dve.wait_ge(slots_psum, 1)
                v.tensor_copy(inv_rms_of[:, :], slots_ps[:, SLOT_TILES:2 * SLOT_TILES])
                link(v.tensor_copy(token_of[:, :], slots_ps[:, 0:SLOT_TILES]))
                v.tensor_scalar(gather_idx[:, :], token_of[:, :], -1.0, 0.0, ALU.add, ALU.max).then_inc(idx_ready, 1)
                link(v.tensor_scalar(skip_add[:, :], token_of[:, :], 0.0, float(OUT_OF_RANGE),
                                     ALU.is_equal, ALU.mult))
                v.scalar_tensor_tensor(out=scatter_idx[:, :], in0=token_of[:, :], scalar=-1.0,
                                       in1=skip_add[:, :], op0=ALU.add, op1=ALU.add).then_inc(idx_ready, 1)

            def mask_scores(n):
                w = width(n % TB)
                dve.wait_ge(score_psum, n + 1)
                v.tensor_scalar(pen[:, n % 2, 0:w], score_bank[n % 3][:, 0:w], 0.0, MASKED,
                                ALU.is_equal, ALU.mult).then_inc(pen_ready, 1)
                dve.wait_ge(pen_ready, n + 1)
                if n >= 3:
                    dve.wait_ge(probT_psum, n - 2)
                v.tensor_tensor_reduce(prob[:, n % 3, 0:w], score_bank[n % 3][:, 0:w], pen[:, n % 2, 0:w],
                                       1.0, MASKED, ALU.add, ALU.max, row_max[:, n:n + 1]
                                       ).then_inc(masked_ready, 1)
                dve.wait_ge(masked_ready, n + 1)
                v.tensor_scalar(neg_max[:, n:n + 1], row_max[:, n:n + 1], MAX_FLOOR, -SCALE,
                                ALU.max, ALU.mult).then_inc(max_ready, 1)

            def finish_attention(b):
                tiles = slice(b * TB, (b + 1) * TB)
                dve.wait_ge(prob_ready, (b + 1) * TB)
                v.reciprocal(row_inv[:, tiles], row_sum[:, tiles]).then_inc(row_inv_ready, 1)
                dve.wait_ge(row_inv_ready, b + 1)
                dve.wait_ge(attn_psum, b + 1)
                v.tensor_tensor(attn[:, tiles, :], attn_bank[:, :].rearrange("p (i d) -> p i d", d=D),
                                row_inv[:, tiles].unsqueeze(2).broadcast_to([P, TB, D]), ALU.mult
                                ).then_inc(attn_ready, 1)

            choose_experts()
            for n in range(NT + 4):
                if n == 2:
                    place_tokens()
                if n == 4:
                    index_slots()
                if n < NT:
                    mask_scores(n)
                if n >= 7 and (n - 7) % TB == 0:
                    finish_attention((n - 7) // TB)

            def step(n, shift):
                t = n - 1
                if exists(t):
                    dve.wait_ge(silu_ready, t + 1 + shift)
                    if t >= 2:
                        dve.wait_ge(hidT_psum, t - 1 + shift)
                    v.tensor_tensor(hid[:, t % 2, :], up_bank[t % 2][:, 0:H], silu_g[:, t % 2, :], ALU.mult
                                    ).then_inc(hid_ready, 1)
                t = n - 3
                if exists(t):
                    dve.wait_ge(down_psum, t + 1 + shift)
                    dve.wait_ge(skip_ready, t + 1 + shift)
                    if t >= 2:
                        dve.wait_ge(gate_ready, t - 1 + shift)
                    v.tensor_tensor(gate_in[:, t % 2, :], down_bank[t % 2][:, 0:D], skip[:, t % RING, :], ALU.add
                                    ).then_inc(gate_in_ready, 1)
                t = n + 1
                if exists(t):
                    dve.wait_ge(rowsT_psum, t + 1 + shift)
                    if t >= 2:
                        dve.wait_ge(up_psum, t - 1 + shift)
                    v.tensor_scalar(rowsT[:, t % 2, :], rowsT_bank[t % 2][:, 0:P], scale[:, 0:1], None, ALU.mult
                                    ).then_inc(rowsT_ready, 1)
                    dve.wait_ge(gathered[t % RING], ring_count(t, shift))
                    if t >= RING:
                        dve.wait_ge(gate_in_ready, t - RING + 1 + shift)
                    col = inv_rms_of[:, t:t + 1] if isinstance(shift, int) else inv_rms_of[:, bass.ds(shift + t, 1)]
                    v.tensor_scalar(skip[:, t % RING, :], rows[:, t % RING, :], col, None, ALU.mult
                                    ).then_inc(skip_ready, 1)

            expert_steps(dve, step)
            for b in range(B):
                tiles = slice(b * TB, (b + 1) * TB)
                dve.wait_ge(gates_loaded[b], 16)
                v.tensor_tensor(fin[:, tiles, :], attn[:, tiles, :], gate_tok[:, tiles, :], ALU.mult
                                ).then_inc(prod_ready, 1)
                dve.wait_ge(prod_ready, b + 1)
                v.tensor_tensor(fin[:, tiles, :], fin[:, tiles, :], x[:, tiles, :], ALU.add).then_inc(fin_ready, 1)

        @block.tensor
        def _(pe):
            m = nc.tensor
            pe.wait_ge(qk_loaded, 32)
            m.matmul(bank[4][:, 0:D], wq[:, :], wk[:, :], start=True, stop=True).then_inc(weights_psum, 1)
            pe.wait_ge(v_loaded, 16)
            pe.wait_ge(ident_made, 3)
            m.transpose(bank[5][:, 0:D], wv[:, :], ident[:, :]).then_inc(weights_psum, 1)
            pe.wait_ge(small_loaded, 32)
            m.transpose(bank[6][:, 0:E], cent[:, :], ident[0:E, 0:E]).then_inc(weights_psum, 1)

            def transpose_tokens(b):
                for i in range(TB):
                    pe.wait_ge(xn_ready, b * TB + i + 1)
                    last = m.transpose(xnT_bank[b][:, i * P:(i + 1) * P], xn[:, b * TB + i, :], ident[:, :])
                last.then_inc(xnT_psum, 1)

            def project_queries(b):
                pe.wait_ge(xnT_ready, b + 1)
                if b == 0:
                    pe.wait_ge(weights_ready, 5)
                if b == 3:
                    pe.wait_ge(zT_ready, 1)
                m.matmul(zT_bank[b][:, :], qk[:, :], xnT[:, b * S:(b + 1) * S], start=True, stop=True
                         ).then_inc(zT_psum, 1)

            def distances(b):
                pe.wait_ge(sq_ready, b + 1)
                for i in range(b * TB, (b + 1) * TB):
                    m.matmul(dist_ps[:, i, 0:E], xnT[:, i * P:(i + 1) * P], centT_scaled[:, :], start=True, stop=True)
                    last = m.matmul(dist_ps[:, i, E:E + 1], xnT_sq[:, i * P:(i + 1) * P], scale_sq[:, :],
                                    start=True, stop=True)
                if b == B - 1:
                    last.then_inc(dist_psum, 1)

            transpose_tokens(0)
            transpose_tokens(1)
            project_queries(0)
            pe.wait_ge(zeroed, 5)
            m.matmul(norm_ps, ones[:, :], centT_sq[:, :], start=True, stop=True)
            distances(0)
            project_queries(1)
            distances(1)
            transpose_tokens(2)
            transpose_tokens(3)
            distances(2)
            distances(3)
            project_queries(2)
            project_queries(3)

            def rank_tokens():
                pe.wait_ge(onehot_ready, 1)
                hot = onehot[:, :, :].rearrange("p e i -> p (e i)")
                m.matmul(rank_ps, before[:, :], hot, start=True, stop=True)
                m.matmul(count_ps, ones_bf[:, :], hot, start=True, stop=True).then_inc(rank_psum, 1)

            def invert_slots():
                pe.wait_ge(hot_ready, 1)
                for i in range(NT):
                    last = m.matmul(slots_ps, hot_lane[:, i, :], hot_val[:, i, :, :].rearrange("p c a -> p (c a)"),
                                    start=(i == 0), stop=(i == NT - 1))
                last.then_inc(slots_psum, 1)

            def scores(n):
                b, q = divmod(n, TB)
                w = width(q)
                if n >= 3:
                    pe.wait_ge(masked_ready, n - 2)
                if q == 0:
                    pe.wait_ge(zT_ready, b + 1)
                m.matmul(score_bank[n % 3][:, 0:w], zT[:, n * P:(n + 1) * P], xnT[:, b * S:b * S + w],
                         start=True, stop=False)
                m.matmul(score_bank[n % 3][:, w - P:w], ident_bf[:, :], causal[:, :], start=False, stop=True
                         ).then_inc(score_psum, 1)

            def transpose_prob(n):
                pe.wait_ge(prob_ready, n + 1)
                if n >= 2:
                    pe.wait_ge(probT_ready, n - 1)
                for j in range(n % TB + 1):
                    last = m.transpose(probT_bank[n % 2][:, j * P:(j + 1) * P], prob[:, n % 3, j * P:(j + 1) * P],
                                       ident[:, :])
                last.then_inc(probT_psum, 1)

            def mix_tokens(b):
                pe.wait_ge(probT_ready, (b + 1) * TB)
                if b >= 1:
                    pe.wait_ge(mixT_ready, b)
                for j in range(TB):
                    last = m.matmul(mixT_bank[:, j * P:S], xn[:, b * TB + j, :], probT[:, b % 2, j, j * P:S],
                                    start=(j == 0), stop=(j == TB - 1))
                last.then_inc(mixT_psum, 1)

            def project_values(b):
                pe.wait_ge(mixT_ready, b + 1)
                if b >= 1:
                    pe.wait_ge(attn_ready, b)
                for i in range(TB):
                    last = m.matmul(attn_bank[:, i * D:(i + 1) * D], mixT[:, b % 2, i * P:(i + 1) * P], wvT[:, :],
                                    start=True, stop=True)
                last.then_inc(attn_psum, 1)

            pe.wait_ge(consts_made, 4)
            for n in range(NT + 4):
                if n == 5:
                    invert_slots()
                if n < NT:
                    scores(n)
                if n == 1:
                    rank_tokens()
                if 0 <= n - 2 < NT:
                    transpose_prob(n - 2)
                if n >= 6 and (n - 6) % TB == 0:
                    mix_tokens((n - 6) // TB)
                if n >= 7 and (n - 7) % TB == 0:
                    project_values((n - 7) // TB)

            pe.wait_ge(expert_ready, 1)
            pe.wait_ge(up_loaded, 16)
            pe.wait_ge(down_loaded, 16)
            pe.wait_ge(attn_ready, B)

            def expert(t, shift):
                col = expert_of[0:1, t:t + 1] if isinstance(shift, int) else expert_of[0:1, bass.ds(shift + t, 1)]
                return pe.value_load(col, min_val=0, max_val=E - 1)

            def step(n, shift):
                t = n
                if exists(t):
                    e = expert(t, shift)
                    pe.wait_ge(rowsT_ready, t + 1 + shift)
                    if t >= 2:
                        pe.wait_ge(hid_ready, t - 1 + shift)
                    m.matmul(up_bank[t % 2][:, :], rowsT[:, t % 2, :], up[:, bass.ds(e * H2, H2)],
                             start=True, stop=True).then_inc(up_psum, 1)
                t = n - 1
                if exists(t):
                    pe.wait_ge(hid_ready, t + 1 + shift)
                    if t >= 2:
                        pe.wait_ge(hidT_ready, t - 1 + shift)
                    for c in range(HC):
                        last = m.transpose(hidT_bank[t % 2][:, c * P:(c + 1) * P], hid[:, t % 2, c * P:(c + 1) * P],
                                           ident[:, :])
                    last.then_inc(hidT_psum, 1)
                t = n + 1
                if exists(t):
                    pe.wait_ge(gathered[t % RING], ring_count(t, shift))
                    if t >= 2:
                        pe.wait_ge(rowsT_ready, t - 1 + shift)
                    m.transpose(rowsT_bank[t % 2][:, 0:P], rows[:, t % RING, :], ident[:, :]).then_inc(rowsT_psum, 1)
                t = n - 2
                if exists(t):
                    e = expert(t, shift)
                    pe.wait_ge(hidT_ready, t + 1 + shift)
                    if t >= 2:
                        pe.wait_ge(gate_in_ready, t - 1 + shift)
                    for c in range(HC):
                        last = m.matmul(down_bank[t % 2][:, 0:D], hidT[:, t % 2, c, :],
                                        down[:, bass.ds(e * H + c * D, D)], start=(c == 0), stop=(c == HC - 1))
                    last.then_inc(down_psum, 1)

            expert_steps(pe, step)


_INS = ["L0_attn_x", "L0_attn_WQ", "L0_attn_WK", "L0_attn_WV",
        "L0_ffn_scale", "L0_ffn_centroids", "L0_ffn_up_w", "L0_ffn_down_w"]


def kernel(**inputs):
    import numpy as _np
    import concourse.bacc as _bacc
    from concourse import mybir as _mybir
    from concourse.bass_utils import run_bass_kernel_spmd as _run

    nc = _bacc.Bacc("TRN2", target_bir_lowering=False, num_devices=1)
    arrays, args = {}, []
    for name in _INS:
        a = _np.ascontiguousarray(inputs[name])
        arrays[f"in_{name}_dram"] = a
        args.append(nc.dram_tensor(f"in_{name}_dram", a.shape, _mybir.dt.from_np(a.dtype), kind="ExternalInput").ap())
    batch, seq, dim = inputs["L0_attn_x"].shape
    out = nc.dram_tensor("out_0_dram", (batch, seq, dim), _mybir.dt.float32, kind="ExternalOutput").ap()
    xf_dram = nc.dram_tensor("xf_dram", (batch * seq, dim), _mybir.dt.float32).ap()
    gate_dram = nc.dram_tensor("gate_dram", (batch * seq, dim), _mybir.dt.float32).ap()
    build(nc, *args, out, xf_dram, gate_dram)
    r = _run(nc, [arrays], core_ids=[0])
    return r.results[0]["out_0_dram"]
```

```python
import concourse.bass as bass
from concourse import mybir
from contextlib import ExitStack

F32 = mybir.dt.float32
BF16 = mybir.dt.bfloat16
I32 = mybir.dt.int32
ALU = mybir.AluOpType
ACT = mybir.ActivationFunctionType
AX = mybir.AxisListType

P = 128
MASKED = -1e30
MAX_FLOOR = -1e29
LN_EPS = 1e-5
RMS_EPS = 1e-6


def build(nc, x_in, wq_in, wk_in, wv_in, scale_in, cent_in, up_in, down_in, out, xf_dram, gate_dram):
    B, S, D = x_in.shape
    E = cent_in.shape[0]
    H = down_in.shape[1]
    H2 = 2 * H
    T = B * S
    NT = T // P
    TB = S // P
    HC = H // P
    PAIRS = NT + E - 1
    PAIR_COLS = -(-PAIRS // 4) * 4
    LAG = E - 1
    SCALE = float(D) ** -0.5
    ROW = D + 1
    assert D == P and S == 512 and H2 == 512 and TB == 4

    x_rows = x_in.rearrange("b s d -> (b s) d")
    x_tiles = x_rows.rearrange("(i p) d -> p i d", p=P)
    out_tiles = out.rearrange("b s d -> (b s) d").rearrange("(i p) d -> p i d", p=P)
    xf_tiles = xf_dram.rearrange("(i p) d -> p i d", p=P)
    gate_tiles = gate_dram.rearrange("(i p) d -> p i d", p=P)

    with ExitStack() as ctx:
        def sb(name, shape, dt=F32):
            return ctx.enter_context(nc.sbuf_tensor(name, shape, dt))

        def sem(name):
            return ctx.enter_context(nc.semaphore(name))

        bank = [ctx.enter_context(nc.psum_tensor(f"bank{n}", [P, 512], F32)) for n in range(8)]

        x = sb("x", [P, NT, D])
        wq, wk, wv = sb("wq", [P, D]), sb("wk", [P, D]), sb("wv", [P, D])
        cent = sb("cent", [E, D])
        scale = sb("scale", [P, 1])
        up = sb("up", [P, E * H2])
        down = sb("down", [P, E * HC * D])
        ident = sb("ident", [P, P])
        scale_row = sb("scale_row", [P, D])
        ident_bf = sb("ident_bf", [P, P], BF16)
        causal = sb("causal", [P, P], BF16)
        not_before = sb("not_before", [P, P], BF16)
        ones_bf = sb("ones_bf", [P, P], BF16)
        ones = sb("ones", [P, P])
        lane_no = sb("lane_no", [P, P, NT], BF16)
        tile_no = sb("tile_no", [P, NT, NT])
        token_no = sb("token_no", [P, NT, 2])
        expert_no = sb("expert_no", [P, E, NT])
        carry_on = sb("carry_on", [P, E, NT])
        pair_no = sb("pair_no", [P, PAIR_COLS, E])
        pair_expert = sb("pair_expert", [P, PAIR_COLS, E])
        lane_col = sb("lane_col", [P, 1])
        table_test = sb("table_test", [P, 1])
        bn = sb("bn", [P, NT, 6])
        st = {n: sb("st_" + n, [P, NT]) for n in
              ("sum", "dif", "m2", "mean", "dsq", "ssq", "var", "inv", "rms2")}
        rad = sb("rad", [P, 2, NT])
        root = sb("root", [P, 2, NT])
        rroot = sb("rroot", [P, 2, NT])
        xn = sb("xn", [P, NT, D])
        xf = sb("xf", [P, NT, ROW])
        xs = sb("xs", [P, NT, D])
        xnT = sb("xnT", [P, T])
        qk = sb("qk", [P, D])
        wvT = sb("wvT", [P, D])
        zT = sb("zT", [P, T])
        pen = sb("pen", [P, 2, S])
        prob = sb("prob", [P, 3, S])
        row_max = sb("row_max", [P, NT])
        neg_max = sb("neg_max", [P, NT])
        row_sum = sb("row_sum", [P, NT])
        row_inv = sb("row_inv", [P, NT])
        probT = sb("probT", [P, 2, TB, S])
        mixT = sb("mixT", [P, 2, S])
        attn = sb("attn", [P, NT, D])
        centT_scaled = sb("centT_scaled", [P, E])
        centT_sq = sb("centT_sq", [P, E])
        xs_sq = sb("xs_sq", [P, 2, D])
        xs_norm, nx = sb("xs_norm", [P, NT]), sb("nx", [P, NT])
        rt = {n: sb("rt_" + n, [P, E, NT]) for n in
              ("dot", "norms", "dist", "eq", "eqw", "cum", "base", "full", "pick")}
        dmin, amin = sb("dmin", [P, NT]), sb("amin", [P, NT])
        onehot = sb("onehot", [P, E, NT], BF16)
        run = sb("run", [P, E + 1])
        run_i = sb("run_i", [P, 2, E], I32)
        run_tiles, used, pairs_of, pairs_end = (sb(n, [P, E]) for n in ("run_tiles", "used", "pairs_of", "pairs_end"))
        pairs_start = sb("pairs_start", [P, E])
        place = sb("place", [P, NT], I32)
        place_lane, place_tile = sb("place_lane", [P, NT], I32), sb("place_tile", [P, NT], I32)
        place_lane_bf = sb("place_lane_bf", [P, NT], BF16)
        hot_lane = sb("hot_lane", [P, P, NT], BF16)
        hot_tile = sb("hot_tile", [P, NT, NT], BF16)
        hot_val = sb("hot_val", [P, NT, 2, NT], BF16)
        token_of = sb("token_of", [P, NT], I32)
        run_of = sb("run_of", [P, 3, E])
        ended = sb("ended", [P, PAIR_COLS, E])
        expert_f = sb("expert_f", [P, PAIR_COLS])
        chosen = sb("chosen", [P, PAIR_COLS, E])
        chosen_run = sb("chosen_run", [P, PAIR_COLS, 3, E])
        pair_run = sb("pair_run", [P, PAIR_COLS, 3])
        tile_f = sb("tile_f", [P, PAIR_COLS])
        bounds = sb("bounds", [P, PAIR_COLS, 2])
        above = sb("above", [P, PAIR_COLS])
        pair_mask = sb("pair_mask", [P, PAIR_COLS])
        expert_c = sb("expert_c", [P, PAIR_COLS])
        weights_of = sb("weights_of", [P, PAIR_COLS, 2], I32)
        tile_of = sb("tile_of", [P, PAIR_COLS], I32)
        rows = sb("rows", [P, NT, ROW])
        cur = sb("cur", [P, 2, D])
        curT = sb("curT", [P, 2, P])
        silu_g = sb("silu_g", [P, 2, H])
        hid = sb("hid", [P, 2, H])
        hidT = sb("hidT", [P, 2, HC, P])
        mixed = sb("mixed", [P, NT, D])
        gate = sb("gate", [P, NT, D])
        gate_tok = sb("gate_tok", [P, NT, D])
        fin = sb("fin", [P, NT, D])

        x_loaded = [sem(f"x_loaded{b}") for b in range(B)]
        qk_loaded, v_loaded, small_loaded = sem("qk_loaded"), sem("v_loaded"), sem("small_loaded")
        scale_row_loaded = sem("scale_row_loaded")
        up_loaded, down_loaded = sem("up_loaded"), sem("down_loaded")
        tables_loaded = sem("tables_loaded")
        zeroed, ident_made, consts_made = sem("zeroed"), sem("ident_made"), sem("consts_made")
        stat_step, rad_ready, root_ready, stats_ready = (
            sem(n) for n in ("stat_step", "rad_ready", "root_ready", "stats_ready"))
        xn_ready, xf_ready = sem("xn_ready"), sem("xf_ready")
        xf_stored = [sem(f"xf_stored{b}") for b in range(B)]
        weights_psum, weights_ready = sem("weights_psum"), sem("weights_ready")
        norms_psum = sem("norms_psum")
        xnT_psum, xnT_ready = sem("xnT_psum"), sem("xnT_ready")
        xs_ready, xs_norm_ready = sem("xs_ready"), sem("xs_norm_ready")
        zT_psum, zT_ready = sem("zT_psum"), sem("zT_ready")
        dist_psum = sem("dist_psum")
        score_psum, pen_ready, masked_ready, max_ready, prob_ready = (
            sem(n) for n in ("score_psum", "pen_ready", "masked_ready", "max_ready", "prob_ready"))
        probT_psum, probT_ready = sem("probT_psum"), sem("probT_ready")
        mixT_psum, mixT_ready = sem("mixT_psum"), sem("mixT_ready")
        attn_psum, attn_ready, row_inv_ready = sem("attn_psum"), sem("attn_ready"), sem("row_inv_ready")
        route_step, onehot_ready, rank_psum = sem("route_step"), sem("onehot_ready"), sem("rank_psum")
        hot_ready, order_psum, order_ready, pairs_ready = (
            sem(n) for n in ("hot_ready", "order_psum", "order_ready", "pairs_ready"))
        gathered = [sem(f"gathered{t}") for t in range(NT)]
        scattered = sem("scattered")
        mixed_begun = sem("mixed_begun")
        cur_ready, curT_psum, curT_ready, up_psum, silu_ready, hid_ready = (
            sem(n) for n in ("cur_ready", "curT_psum", "curT_ready", "up_psum", "silu_ready", "hid_ready"))
        hidT_psum, hidT_ready, down_psum, mixed_ready, gate_ready = (
            sem(n) for n in ("hidT_psum", "hidT_ready", "down_psum", "mixed_ready", "gate_ready"))
        gates_loaded = [sem(f"gates_loaded{b}") for b in range(B)]
        prod_ready, fin_ready, stored = sem("prod_ready"), sem("fin_ready"), sem("stored")

        xnT_bank = bank[0:4]
        zT_bank = [bank[4], bank[5], bank[6], bank[4]]
        route_bank = bank[7]
        dist_ps = route_bank[:, 0:NT * 16].rearrange("p (i c) -> p i c", c=16)
        norm_ps = route_bank[:, 256:256 + E]
        rank_ps = route_bank[:, 0:E * NT]
        count_ps = route_bank[:, E * NT:2 * E * NT]
        order_ps = route_bank[:, 256:256 + 2 * NT]
        score_bank = bank[0:3]
        probT_bank = bank[3:5]
        mixT_bank, attn_bank = bank[5], bank[6]
        up_bank = bank[0:2]
        hidT_bank = bank[2:4]
        curT_bank = [bank[4], bank[7]]
        down_bank = bank[5:7]

        EARLY = (B - 1) * TB

        def width(q):
            return (q + 1) * P

        GATE_LAG = LAG + 4
        STEPS = range(-2, NT + GATE_LAG)
        CHUNK = 4
        assert PAIRS <= PAIR_COLS and PAIR_COLS % CHUNK == 0

        def exists(p):
            return 0 <= p < PAIRS

        def load_numbers(eng, table, name, c, per_pair, most):
            regs = [eng.alloc_register(f"{name}{c * CHUNK + i // per_pair}_{i % per_pair}")
                    for i in range(CHUNK * per_pair)]
            eng.load(regs, table[0:1, c * CHUNK * per_pair:(c + 1) * CHUNK * per_pair])
            return [eng.snap(r, donate=True, min_val=0, max_val=most[i % per_pair]) for i, r in enumerate(regs)]

        def tile_at(t, tile):
            return t[:, bass.ds(tile, 1), :].rearrange("p a d -> p (a d)")

        block = ctx.enter_context(nc.Block())

        @block.sync
        def _(sp):
            for b in range(B):
                sp.dma_start(x[:, b * TB:(b + 1) * TB, :], x_tiles[:, b * TB:(b + 1) * TB, :]
                             ).then_inc(x_loaded[b], 16)
            sp.dma_start(wq[:, :], wq_in).then_inc(qk_loaded, 16)
            sp.dma_start(wk[:, :], wk_in).then_inc(qk_loaded, 16)
            sp.dma_start(cent[:, :], cent_in).then_inc(small_loaded, 16)
            sp.dma_start(scale[:, :], scale_in.rearrange("(p a) -> p a", a=1)).then_inc(small_loaded, 16)
            sp.dma_start(wv[:, :], wv_in).then_inc(v_loaded, 16)
            sp.dma_start(scale_row[:, :], scale_in.rearrange("(a d) -> a d", a=1).broadcast_to([P, D])
                         ).then_inc(scale_row_loaded, 16)
            sp.dma_start(up[:, :].rearrange("p (e n) -> p e n", e=E), up_in.rearrange("e d h -> d e h")
                         ).then_inc(up_loaded, 16)
            sp.dma_start(down[:, :].rearrange("p (e c n) -> p e c n", e=E, c=HC),
                         down_in.rearrange("e (c p) d -> p e c d", p=P)).then_inc(down_loaded, 16)
            for b in range(B):
                sp.wait_ge(xf_ready, (b + 1) * (TB + 1))
                sp.dma_start(xf_tiles[:, b * TB:(b + 1) * TB, :], xf[:, b * TB:(b + 1) * TB, :]
                             ).then_inc(xf_stored[b], 16)
            sp.wait_ge(scattered, 16 * NT)
            for b in range(B):
                sp.dma_start(gate_tok[:, b * TB:(b + 1) * TB, :], gate_tiles[:, b * TB:(b + 1) * TB, :]
                             ).then_inc(gates_loaded[b], 16)
            for b in range(B):
                sp.wait_ge(fin_ready, b + 1)
                sp.dma_start(out_tiles[:, b * TB:(b + 1) * TB, :], fin[:, b * TB:(b + 1) * TB, :]
                             ).then_inc(stored, 16)
            sp.wait_ge(stored, 16 * B)

        @block.gpsimd
        def _(pool):
            g = nc.gpsimd
            g.memset(ident[:, :], 0.0).then_inc(zeroed, 1)
            g.memset(ident_bf[:, :], 0.0).then_inc(zeroed, 1)
            g.memset(causal[:, :], 0.0).then_inc(zeroed, 1)
            g.memset(not_before[:, :], -1.0).then_inc(zeroed, 1)
            g.memset(ones[:, :], 1.0).then_inc(zeroed, 1)
            pool.wait_ge(zeroed, 5)
            g.affine_select(out=ident[:, :], in_=ident[:, :], compare_op=ALU.not_equal, fill=1.0, base=0,
                            pattern=[[-1, P]], channel_multiplier=1).then_inc(ident_made, 1)
            g.affine_select(out=ident_bf[:, :], in_=ident_bf[:, :], compare_op=ALU.not_equal, fill=1.0,
                            base=0, pattern=[[-1, P]], channel_multiplier=1).then_inc(ident_made, 1)
            g.affine_select(out=causal[:, :], in_=causal[:, :], compare_op=ALU.is_ge, fill=MASKED, base=0,
                            pattern=[[-1, P]], channel_multiplier=1).then_inc(ident_made, 1)
            g.affine_select(out=not_before[:, :], in_=not_before[:, :], compare_op=ALU.is_ge, fill=0.0, base=0,
                            pattern=[[-1, P]], channel_multiplier=1).then_inc(consts_made, 1)
            g.memset(ones_bf[:, :], 1.0).then_inc(consts_made, 1)
            g.memset(carry_on[:, :, 1:NT], 1.0).then_inc(consts_made, 1)
            g.memset(carry_on[:, :, 0:1], 0.0).then_inc(consts_made, 1)
            g.memset(run[:, 0:1], 0.0).then_inc(consts_made, 1)

            def count(dst, pattern, base, lanes):
                g.iota(dst, pattern=pattern, base=base, channel_multiplier=lanes,
                       allow_small_or_imprecise_dtypes=True).then_inc(consts_made, 1)

            count(expert_no[:, :, :], [[1, E], [0, NT]], -E, 0)
            count(lane_no[:, :, :], [[1, P], [0, NT]], 0, 0)
            count(tile_no[:, :, :], [[0, NT], [1, NT]], 0, 0)
            count(token_no[:, :, 0:1], [[P, NT]], 0, 0)
            count(token_no[:, :, 1:2], [[0, NT]], 0, 1)
            count(pair_no[:, :, :], [[1, PAIR_COLS], [0, E]], 0, 0)
            count(pair_expert[:, :, :], [[0, PAIR_COLS], [1, E]], 0, 0)
            count(lane_col[:, :], [[0, 1]], 0, 1)
            pool.wait_ge(scale_row_loaded, 16)
            for b in range(B):
                tiles = slice(b * TB, (b + 1) * TB)
                pool.wait_ge(xn_ready, (b + 1) * TB)
                g.tensor_tensor(xs[:, tiles, :], xn[:, tiles, :],
                                scale_row[:, :].unsqueeze(1).broadcast_to([P, TB, D]), ALU.mult
                                ).then_inc(xs_ready, 1)
            for b in range(B):
                for i in range(b * TB, (b + 1) * TB):
                    g.tensor_scalar(xf[:, i, 0:D], xn[:, i, :], rroot[:, 1, i:i + 1], 1.0, ALU.mult, ALU.mult
                                    ).then_inc(xf_ready, 1)
                g.tensor_copy(xf[:, b * TB:(b + 1) * TB, D:ROW],
                              root[:, 1, b * TB:(b + 1) * TB].unsqueeze(2)).then_inc(xf_ready, 1)
            for b in range(B):
                pool.wait_ge(xf_stored[b], 16)
            pool.wait_ge(order_ready, 1)
            AHEAD = 3
            for t in range(NT + AHEAD):
                if t < NT:
                    g.indirect_dma_start(rows[:, t, :], None, xf_dram,
                                         bass.IndirectOffsetOnAxis(token_of[:, t:t + 1], 0)
                                         ).then_inc(gathered[t], 16)
                if t >= AHEAD:
                    u = t - AHEAD
                    pool.wait_ge(gathered[u], 16)
                    g.tensor_scalar(mixed[:, u, :], rows[:, u, 0:D], rows[:, u, D:ROW], 1.0, ALU.mult, ALU.mult
                                    ).then_inc(mixed_begun, 1)
            for t in range(NT):
                pool.wait_ge(gate_ready, t + 1)
                g.indirect_dma_start(gate_dram, bass.IndirectOffsetOnAxis(token_of[:, t:t + 1], 0),
                                     gate[:, t, :], None).then_inc(scattered, 16)

        @block.scalar
        def _(act):
            a = nc.scalar
            def load_table(func):
                a.activation(table_test[:, :], ones[:, 0:1], func).then_inc(tables_loaded, 1)

            def copy_z(b):
                act.wait_ge(zT_psum, b + 1)
                a.activation(zT[:, b * S:(b + 1) * S], zT_bank[b][:, :], ACT.Copy).then_inc(zT_ready, 1)

            def copy_probT(n):
                b, q = divmod(n, TB)
                act.wait_ge(probT_psum, n + 1)
                if q == 0 and b >= 2:
                    act.wait_ge(mixT_psum, b - 1)
                a.activation(probT[:, b % 2, 0:q + 1, q * P:(q + 1) * P],
                                     probT_bank[n % 2][:, 0:width(q)].rearrange("p (j c) -> p j c", c=P),
                                     ACT.Copy).then_inc(probT_ready, 1)

            def copy_mix(b):
                act.wait_ge(mixT_psum, b + 1)
                if b >= 2:
                    act.wait_ge(attn_psum, b - 1)
                a.activation(mixT[:, b % 2, :], mixT_bank[:, :], ACT.Copy).then_inc(mixT_ready, 1)

            act.wait_ge(zeroed, 5)
            load_table(ACT.Sqrt)
            act.wait_ge(rad_ready, 1)
            a.activation(root[:, :, :], rad[:, :, :], ACT.Sqrt).then_inc(root_ready, 1)
            act.wait_ge(tables_loaded, 1)
            load_table(ACT.Exp)
            act.wait_ge(weights_psum, 3)
            act.wait_ge(small_loaded, 32)
            a.activation(centT_scaled[:, :], bank[6][:, 0:E], ACT.Identity, bias=0.0,
                         scale=scale[:, 0:1]).then_inc(weights_ready, 1)
            a.activation(centT_sq[:, :], bank[6][:, 0:E], ACT.Square).then_inc(weights_ready, 1)
            a.activation(qk[:, :], bank[4][:, 0:D], ACT.Copy).then_inc(weights_ready, 1)
            a.activation(wvT[:, :], bank[5][:, 0:D], ACT.Copy).then_inc(weights_ready, 1)

            def copy_xT(b):
                act.wait_ge(xnT_psum, b + 1)
                a.activation(xnT[:, b * S:(b + 1) * S], xnT_bank[b][:, :], ACT.Copy).then_inc(xnT_ready, 1)

            def norms(b):
                act.wait_ge(xs_ready, b + 1)
                for i in range(b * TB, (b + 1) * TB):
                    if i >= 2:
                        act.wait_ge(xs_norm_ready, i - 1)
                    a.activation(xs_sq[:, i % 2, :], xs[:, i, :], ACT.Square, accum_out=xs_norm[:, i:i + 1]
                                 ).then_inc(xs_norm_ready, 1)

            copy_xT(0)
            copy_xT(1)
            norms(0)
            copy_xT(2)
            norms(1)
            copy_xT(3)
            norms(2)
            norms(3)
            for b in range(B):
                copy_z(b)

            def exps(first, end):
                for n in range(first, end + 3):
                    if n < end:
                        w = width(n % TB)
                        act.wait_ge(max_ready, n + 1)
                        a.activation(prob[:, n % 3, 0:w], prob[:, n % 3, 0:w], ACT.Exp, bias=neg_max[:, n:n + 1],
                                     scale=SCALE, accum_out=row_sum[:, n:n + 1]).then_inc(prob_ready, 1)
                    if first <= n - 2 < end:
                        copy_probT(n - 2)
                    if n - 3 >= first and (n - 3) % TB == TB - 1:
                        copy_mix((n - 3) // TB)

            exps(0, EARLY)
            act.wait_ge(tables_loaded, 2)

            def step(n):
                t = n
                if exists(t):
                    act.wait_ge(up_psum, t + 1)
                    if t >= 2:
                        act.wait_ge(hid_ready, t - 1)
                    a.activation(silu_g[:, t % 2, :], up_bank[t % 2][:, H:H2], ACT.Silu).then_inc(silu_ready, 1)
                if 0 <= n - GATE_LAG < NT:
                    act.wait_ge(mixed_ready, n - GATE_LAG + LAG + 1)
                t = n - 1
                if exists(t):
                    act.wait_ge(hidT_psum, t + 1)
                    if t >= 2:
                        act.wait_ge(down_psum, t - 1)
                    a.activation(hidT[:, t % 2, :, :], hidT_bank[t % 2][:, 0:H].rearrange("p (c j) -> p c j", c=HC),
                                 ACT.Copy).then_inc(hidT_ready, 1)
                t = n - GATE_LAG
                if 0 <= t < NT:
                    a.activation(gate[:, t, :], mixed[:, t, :], ACT.Silu).then_inc(gate_ready, 1)

            load_table(ACT.Silu)
            for n in STEPS:
                step(n)
            act.wait_ge(tables_loaded, 3)
            load_table(ACT.Exp)
            exps(EARLY, NT)

        @block.vector
        def _(dve):
            v = nc.vector
            steps = [0]

            def link(ins):
                steps[0] += 1
                ins.then_inc(stat_step, 1)
                dve.wait_ge(stat_step, steps[0])

            def moments(b):
                dve.wait_ge(x_loaded[b], 16)
                for i in range(b * TB, (b + 1) * TB):
                    last = v.bn_stats(bn[:, i, :], x[:, i, :])
                if b == B - 1:
                    link(last)

            def statistics():
                s_ = {n: t[:, :] for n, t in st.items()}
                mean_e, m2_e, mean_o, m2_o = (bn[:, :, c] for c in (1, 2, 4, 5))
                v.tensor_tensor(s_["sum"], mean_e, mean_o, ALU.add)
                v.tensor_tensor(s_["m2"], m2_e, m2_o, ALU.add)
                link(v.tensor_tensor(s_["dif"], mean_e, mean_o, ALU.subtract))
                link(v.tensor_tensor(s_["dsq"], s_["dif"], s_["dif"], ALU.mult))
                link(v.scalar_tensor_tensor(out=s_["ssq"], in0=s_["dsq"], scalar=D / 4, in1=s_["m2"],
                                            op0=ALU.mult, op1=ALU.add))
                v.tensor_scalar(s_["var"], s_["ssq"], 1.0 / D, None, ALU.mult)
                link(v.tensor_scalar(rad[:, 0, :], s_["ssq"], 1.0 / D, LN_EPS, ALU.mult, ALU.add))
                link(v.reciprocal(s_["inv"], rad[:, 0, :]))
                link(v.tensor_tensor(s_["dif"], s_["var"], s_["inv"], ALU.mult))
                v.tensor_scalar(rad[:, 1, :], s_["dif"], RMS_EPS, None, ALU.add).then_inc(rad_ready, 1)
                link(v.tensor_scalar(s_["mean"], s_["sum"], 0.5, None, ALU.mult))

            def normalise():
                dve.wait_ge(root_ready, 1)
                link(v.reciprocal(rroot[:, :, :], root[:, :, :]))
                v.tensor_tensor(st["rms2"][:, :], rroot[:, 1, :], rroot[:, 1, :], ALU.mult).then_inc(stats_ready, 1)
                for i in range(NT):
                    v.tensor_scalar(xn[:, i, :], x[:, i, :], st["mean"][:, i:i + 1], rroot[:, 0, i:i + 1],
                                    ALU.subtract, ALU.mult).then_inc(xn_ready, 1)

            for b in range(B):
                moments(b)
            statistics()
            normalise()

            def over_tiles(ap):
                return ap.unsqueeze(2).broadcast_to([P, E, NT])

            def over_experts(ap):
                return ap.unsqueeze(1).broadcast_to([P, E, NT])

            def choose_experts():
                dve.wait_ge(consts_made, 13)
                dve.wait_ge(stats_ready, 1)
                dve.wait_ge(xs_norm_ready, NT)
                link(v.tensor_tensor(nx[:, :], xs_norm[:, :], st["rms2"][:, :], ALU.mult))
                dve.wait_ge(dist_psum, 1)
                link(v.tensor_tensor(rt["norms"][:, :, :], over_experts(nx[:, :]), over_tiles(norm_ps), ALU.add))
                link(v.scalar_tensor_tensor(out=rt["dot"][:, :, :],
                                            in0=dist_ps[:, :, 0:E].rearrange("p i e -> p e i"), scalar=-2.0,
                                            in1=over_experts(rroot[:, 1, :]), op0=ALU.mult, op1=ALU.mult))
                link(v.tensor_tensor(rt["dist"][:, :, :], rt["norms"][:, :, :], rt["dot"][:, :, :], ALU.add))
                link(v.tensor_reduce(dmin[:, :], rt["dist"][:, :, :].rearrange("p e i -> p i e"), AX.X, ALU.min))
                link(v.tensor_tensor(rt["eq"][:, :, :], rt["dist"][:, :, :], over_experts(dmin[:, :]), ALU.is_equal))
                link(v.tensor_tensor(rt["eqw"][:, :, :], rt["eq"][:, :, :], expert_no[:, :, :], ALU.mult))
                link(v.tensor_reduce(amin[:, :], rt["eqw"][:, :, :].rearrange("p e i -> p i e"), AX.X, ALU.min))
                v.tensor_tensor(onehot[:, :, :], expert_no[:, :, :], over_experts(amin[:, :]), ALU.is_equal
                                ).then_inc(onehot_ready, 1)

            def place_tokens():
                flat = "p e i -> p (e i)"
                dve.wait_ge(rank_psum, 1)
                link(v.tensor_tensor_scan(rt["cum"][:, :, :].rearrange(flat), carry_on[:, :, :].rearrange(flat),
                                          count_ps, 0.0, ALU.mult, ALU.add))
                link(v.tensor_tensor_scan(run[:, 1:E + 1], ones[:, 0:E], rt["cum"][:, :, NT - 1], 0.0,
                                          ALU.mult, ALU.add))
                link(v.tensor_tensor(rt["base"][:, :, :], over_tiles(run[:, 0:E]), rt["cum"][:, :, :], ALU.add))
                link(v.tensor_tensor(rt["full"][:, :, :].rearrange(flat), rt["base"][:, :, :].rearrange(flat),
                                     rank_ps, ALU.add))
                link(v.tensor_tensor(rt["pick"][:, :, :], rt["full"][:, :, :], onehot[:, :, :], ALU.mult))
                with nc.allow_low_precision(reason="places are whole numbers below 2^24"):
                    link(v.tensor_reduce(place[:, :], rt["pick"][:, :, :].rearrange("p e i -> p i e"), AX.X, ALU.add))
                link(v.tensor_scalar(place_lane[:, :], place[:, :], P - 1, None, ALU.bitwise_and))
                v.tensor_scalar(place_tile[:, :], place[:, :], 7, None, ALU.logical_shift_right)
                link(v.tensor_copy(place_lane_bf[:, :], place_lane[:, :]))
                v.tensor_tensor(hot_lane[:, :, :], place_lane_bf[:, :].unsqueeze(1).broadcast_to([P, P, NT]),
                                lane_no[:, :, :], ALU.is_equal).then_inc(hot_ready, 1)
                link(v.tensor_tensor(hot_tile[:, :, :], place_tile[:, :].unsqueeze(2).broadcast_to([P, NT, NT]),
                                     tile_no[:, :, :], ALU.is_equal))
                v.tensor_tensor(hot_val[:, :, :, :], hot_tile[:, :, :].unsqueeze(2).broadcast_to([P, NT, 2, NT]),
                                token_no[:, :, :].unsqueeze(3).broadcast_to([P, NT, 2, NT]), ALU.mult
                                ).then_inc(hot_ready, 1)

            def read_order():
                dve.wait_ge(order_psum, 1)
                with nc.allow_low_precision(reason="tokens are whole numbers below 2^24"):
                    v.tensor_reduce(token_of[:, :], order_ps.rearrange("p (c a) -> p a c", c=2), AX.X, ALU.add
                                    ).then_inc(order_ready, 1)

            def list_pairs():
                start, end = run[:, 0:E], run[:, 1:E + 1]
                v.tensor_copy(run_i[:, 0, :], start)
                v.tensor_copy(run_of[:, 0, :], start)
                v.tensor_copy(run_of[:, 1, :], end)
                v.tensor_tensor(used[:, :], end, start, ALU.is_gt)
                link(v.tensor_scalar(run_i[:, 1, :], end, float(P - 1), None, ALU.add))
                link(v.tensor_scalar(run_i[:, :, :], run_i[:, :, :], 7, None, ALU.logical_shift_right))
                link(v.tensor_tensor(run_tiles[:, :], run_i[:, 1, :], run_i[:, 0, :], ALU.subtract))
                link(v.tensor_tensor(pairs_of[:, :], run_tiles[:, :], used[:, :], ALU.mult))
                link(v.tensor_tensor_scan(pairs_end[:, :], ones[:, 0:E], pairs_of[:, :], 0.0, ALU.mult, ALU.add))
                link(v.tensor_tensor(pairs_start[:, :], pairs_end[:, :], pairs_of[:, :], ALU.subtract))
                v.tensor_tensor(run_of[:, 2, :], run_i[:, 0, :], pairs_start[:, :], ALU.subtract)

            def list_pairs_2():
                shape = [P, PAIR_COLS, E]
                link(v.tensor_tensor(ended[:, :, :], pairs_end[:, :].unsqueeze(1).broadcast_to(shape),
                                     pair_no[:, :, :], ALU.is_le))
                link(v.tensor_reduce(expert_f[:, :], ended[:, :, :], AX.X, ALU.add))
                v.tensor_scalar(expert_c[:, :], expert_f[:, :], float(E - 1), None, ALU.min)
                link(v.tensor_tensor(chosen[:, :, :], expert_f[:, :].unsqueeze(2).broadcast_to(shape),
                                     pair_expert[:, :, :], ALU.is_equal))
                link(v.tensor_tensor(chosen_run[:, :, :, :], chosen[:, :, :].unsqueeze(2).broadcast_to([P, PAIR_COLS, 3, E]),
                                     run_of[:, :, :].unsqueeze(1).broadcast_to([P, PAIR_COLS, 3, E]), ALU.mult))
                link(v.tensor_reduce(pair_run[:, :, :], chosen_run[:, :, :, :], AX.X, ALU.add))

            def list_pairs_3():
                link(v.tensor_tensor(tile_f[:, :], pair_run[:, :, 2], pair_no[:, :, 0], ALU.add))
                link(v.tensor_scalar(tile_f[:, :], tile_f[:, :], float(NT - 1), None, ALU.min))
                v.tensor_copy(tile_of[:, :], tile_f[:, :])
                v.tensor_scalar(weights_of[:, :, 0], expert_c[:, :], float(H2), None, ALU.mult)
                v.tensor_scalar(weights_of[:, :, 1], expert_c[:, :], float(H), None, ALU.mult)
                link(v.scalar_tensor_tensor(out=bounds[:, :, :], in0=tile_f[:, :].unsqueeze(2).broadcast_to([P, PAIR_COLS, 2]),
                                            scalar=-float(P), in1=pair_run[:, :, 0:2], op0=ALU.mult, op1=ALU.add))
                link(v.tensor_scalar(above[:, :], bounds[:, :, 0], lane_col[:, 0:1], None, ALU.is_le))
                link(v.scalar_tensor_tensor(out=pair_mask[:, :], in0=bounds[:, :, 1], scalar=lane_col[:, 0:1],
                                            in1=above[:, :], op0=ALU.is_gt, op1=ALU.mult))
                v.engine_nop().then_inc(pairs_ready, 1)

            def mask_scores(n):
                w = width(n % TB)
                dve.wait_ge(score_psum, n + 1)
                v.tensor_scalar(pen[:, n % 2, 0:w], score_bank[n % 3][:, 0:w], 0.0, MASKED,
                                ALU.is_equal, ALU.mult).then_inc(pen_ready, 1)
                dve.wait_ge(pen_ready, n + 1)
                if n >= 3:
                    dve.wait_ge(probT_psum, n - 2)
                v.tensor_tensor_reduce(prob[:, n % 3, 0:w], score_bank[n % 3][:, 0:w], pen[:, n % 2, 0:w],
                                       1.0, MASKED, ALU.add, ALU.max, row_max[:, n:n + 1]
                                       ).then_inc(masked_ready, 1)
                dve.wait_ge(masked_ready, n + 1)
                v.tensor_scalar(neg_max[:, n:n + 1], row_max[:, n:n + 1], MAX_FLOOR, -SCALE,
                                ALU.max, ALU.mult).then_inc(max_ready, 1)

            def finish_attention(b):
                tiles = slice(b * TB, (b + 1) * TB)
                dve.wait_ge(prob_ready, (b + 1) * TB)
                v.reciprocal(row_inv[:, tiles], row_sum[:, tiles]).then_inc(row_inv_ready, 1)
                dve.wait_ge(row_inv_ready, b + 1)
                dve.wait_ge(attn_psum, b + 1)
                v.tensor_tensor(attn[:, tiles, :], attn_bank[:, :].rearrange("p (i d) -> p i d", d=D),
                                row_inv[:, tiles].unsqueeze(2).broadcast_to([P, TB, D]), ALU.mult
                                ).then_inc(attn_ready, 1)

            def attend(first, end, between={}):
                for n in range(first, end + 4):
                    for part in between.get(n, ()):
                        part()
                    if n < end:
                        mask_scores(n)
                    if n - 4 >= first and (n - 4) % TB == TB - 1:
                        finish_attention((n - 4) // TB)

            choose_experts()
            attend(0, EARLY, {2: [place_tokens], 4: [read_order], 7: [list_pairs], 8: [list_pairs_2], 9: [list_pairs_3]})
            tiles = []

            def step(n):
                t = n - 1
                if exists(t):
                    dve.wait_ge(silu_ready, t + 1)
                    if t >= 2:
                        dve.wait_ge(hidT_psum, t - 1)
                    v.tensor_tensor(hid[:, t % 2, :], up_bank[t % 2][:, 0:H], silu_g[:, t % 2, :], ALU.mult
                                    ).then_inc(hid_ready, 1)
                t = n - 3
                if exists(t):
                    tile = tiles[t]
                    dve.wait_ge(down_psum, t + 1)
                    if t >= 1:
                        dve.wait_ge(mixed_ready, t)
                    v.scalar_tensor_tensor(out=tile_at(mixed, tile), in0=down_bank[t % 2][:, 0:D],
                                           scalar=pair_mask[:, t:t + 1], in1=tile_at(mixed, tile),
                                           op0=ALU.mult, op1=ALU.add).then_inc(mixed_ready, 1)
                t = n + 1
                if exists(t):
                    dve.wait_ge(curT_psum, t + 1)
                    if t >= 2:
                        dve.wait_ge(up_psum, t - 1)
                    v.tensor_scalar(curT[:, t % 2, :], curT_bank[t % 2][:, 0:P], scale[:, 0:1], None, ALU.mult
                                    ).then_inc(curT_ready, 1)
                t = n + 2
                if exists(t):
                    if t % CHUNK == 0:
                        tiles.extend(load_numbers(dve, tile_of, "tile", t // CHUNK, 1, [NT - 1]))
                    tile = tiles[t]
                    dve.wait_ge(mixed_begun, min(t, NT - 1) + 1)
                    if t >= 2:
                        dve.wait_ge(curT_psum, t - 1)
                    v.tensor_copy(cur[:, t % 2, :], tile_at(rows, tile)[:, 0:D]).then_inc(cur_ready, 1)

            for n in STEPS:
                step(n)
            attend(EARLY, NT)
            for b in range(B):
                tiles = slice(b * TB, (b + 1) * TB)
                dve.wait_ge(gates_loaded[b], 16)
                v.tensor_tensor(fin[:, tiles, :], attn[:, tiles, :], gate_tok[:, tiles, :], ALU.mult
                                ).then_inc(prod_ready, 1)
                dve.wait_ge(prod_ready, b + 1)
                v.tensor_tensor(fin[:, tiles, :], fin[:, tiles, :], x[:, tiles, :], ALU.add).then_inc(fin_ready, 1)

        @block.tensor
        def _(pe):
            m = nc.tensor
            def keep_busy(turns):
                with pe.Fori(0, turns) as _:
                    for _ in range(8):
                        m.matmul(bank[7][:, 0:P], ident_bf[:, :], ident_bf[:, :], start=True, stop=True)

            pe.wait_ge(ident_made, 3)
            keep_busy(4)
            pe.wait_ge(small_loaded, 32)
            m.transpose(bank[6][:, 0:E], cent[:, :], ident[0:E, 0:E]).then_inc(weights_psum, 1)
            pe.wait_ge(qk_loaded, 32)
            m.matmul(bank[4][:, 0:D], wq[:, :], wk[:, :], start=True, stop=True).then_inc(weights_psum, 1)
            pe.wait_ge(v_loaded, 16)
            m.transpose(bank[5][:, 0:D], wv[:, :], ident[:, :]).then_inc(weights_psum, 1)
            keep_busy(4)

            def transpose_tokens(b):
                for i in range(TB):
                    pe.wait_ge(xn_ready, b * TB + i + 1)
                    last = m.transpose(xnT_bank[b][:, i * P:(i + 1) * P], xn[:, b * TB + i, :], ident[:, :])
                last.then_inc(xnT_psum, 1)

            def project_queries(b):
                pe.wait_ge(xnT_ready, b + 1)
                if b == 0:
                    pe.wait_ge(weights_ready, 4)
                if b == 3:
                    pe.wait_ge(zT_ready, 1)
                m.matmul(zT_bank[b][:, :], qk[:, :], xnT[:, b * S:(b + 1) * S], start=True, stop=True
                         ).then_inc(zT_psum, 1)

            def distances(b):
                pe.wait_ge(xnT_ready, b + 1)
                if b == 0:
                    pe.wait_ge(weights_ready, 4)
                for i in range(b * TB, (b + 1) * TB):
                    last = m.matmul(dist_ps[:, i, 0:E], xnT[:, i * P:(i + 1) * P], centT_scaled[:, :], start=True, stop=True)
                if b == B - 1:
                    last.then_inc(dist_psum, 1)

            transpose_tokens(0)
            transpose_tokens(1)
            distances(0)
            m.matmul(norm_ps, ones[:, :], centT_sq[:, :], start=True, stop=True)
            distances(1)
            transpose_tokens(2)
            project_queries(0)
            transpose_tokens(3)
            distances(2)
            distances(3)
            for b in range(1, B):
                project_queries(b)

            def rank_tokens():
                pe.wait_ge(onehot_ready, 1)
                hot = onehot[:, :, :].rearrange("p e i -> p (e i)")
                m.matmul(rank_ps, not_before[:, :], hot, start=True, stop=True)
                m.matmul(count_ps, ones_bf[:, :], hot, start=True, stop=True).then_inc(rank_psum, 1)

            def invert_order():
                pe.wait_ge(hot_ready, 2)
                for i in range(NT):
                    last = m.matmul(order_ps, hot_lane[:, :, i], hot_val[:, i, :, :].rearrange("p c a -> p (c a)"),
                                    start=(i == 0), stop=(i == NT - 1))
                last.then_inc(order_psum, 1)

            def scores(n):
                b, q = divmod(n, TB)
                w = width(q)
                if n >= 3:
                    pe.wait_ge(masked_ready, n - 2)
                if q == 0:
                    pe.wait_ge(zT_ready, b + 1)
                m.matmul(score_bank[n % 3][:, 0:w], zT[:, n * P:(n + 1) * P], xnT[:, b * S:b * S + w],
                         start=True, stop=False)
                m.matmul(score_bank[n % 3][:, w - P:w], ident_bf[:, :], causal[:, :], start=False, stop=True
                         ).then_inc(score_psum, 1)

            def transpose_prob(n):
                pe.wait_ge(prob_ready, n + 1)
                if n >= 2:
                    pe.wait_ge(probT_ready, n - 1)
                for j in range(n % TB + 1):
                    last = m.transpose(probT_bank[n % 2][:, j * P:(j + 1) * P], prob[:, n % 3, j * P:(j + 1) * P],
                                       ident[:, :])
                last.then_inc(probT_psum, 1)

            def mix_tokens(b):
                pe.wait_ge(probT_ready, (b + 1) * TB)
                if b >= 1:
                    pe.wait_ge(mixT_ready, b)
                for j in range(TB):
                    last = m.matmul(mixT_bank[:, j * P:S], xn[:, b * TB + j, :], probT[:, b % 2, j, j * P:S],
                                    start=(j == 0), stop=(j == TB - 1))
                last.then_inc(mixT_psum, 1)

            def project_values(b):
                pe.wait_ge(mixT_ready, b + 1)
                if b >= 1:
                    pe.wait_ge(attn_ready, b)
                for i in range(TB):
                    last = m.matmul(attn_bank[:, i * D:(i + 1) * D], mixT[:, b % 2, i * P:(i + 1) * P], wvT[:, :],
                                    start=True, stop=True)
                last.then_inc(attn_psum, 1)

            def attend(first, end, between={}):
                for n in range(first, end + 4):
                    for part in between.get(n, ()):
                        part()
                    if n < end:
                        scores(n)
                    if first <= n - 2 < end:
                        transpose_prob(n - 2)
                    if n - 3 >= first and (n - 3) % TB == TB - 1:
                        mix_tokens((n - 3) // TB)
                    if n - 4 >= first and (n - 4) % TB == TB - 1:
                        project_values((n - 4) // TB)

            pe.wait_ge(consts_made, 2)
            attend(0, EARLY, {2: [rank_tokens], 5: [invert_order]})
            pe.wait_ge(pairs_ready, 1)
            pe.wait_ge(up_loaded, 16)
            pe.wait_ge(down_loaded, 16)
            pe.wait_ge(probT_ready, EARLY)

            weights_flat = weights_of[:, :, :].rearrange("p n k -> p (n k)")
            starts = []

            def step(n):
                t = n
                if exists(t):
                    pe.wait_ge(curT_ready, t + 1)
                    if t >= 2:
                        pe.wait_ge(hid_ready, t - 1)
                    m.matmul(up_bank[t % 2][:, :], curT[:, t % 2, :], up[:, bass.ds(starts[2 * t], H2)],
                             start=True, stop=True).then_inc(up_psum, 1)
                if exists(n + 2) and (n + 2) % CHUNK == 0:
                    starts.extend(load_numbers(pe, weights_flat, "start", (n + 2) // CHUNK, 2,
                                               [(E - 1) * H2, (E - 1) * H]))
                t = n - 1
                if exists(t):
                    pe.wait_ge(hid_ready, t + 1)
                    if t >= 2:
                        pe.wait_ge(hidT_ready, t - 1)
                    for c in range(HC):
                        last = m.transpose(hidT_bank[t % 2][:, c * P:(c + 1) * P], hid[:, t % 2, c * P:(c + 1) * P],
                                           ident[:, :])
                    last.then_inc(hidT_psum, 1)
                t = n + 1
                if exists(t):
                    pe.wait_ge(cur_ready, t + 1)
                    if t >= 2:
                        pe.wait_ge(curT_ready, t - 1)
                    m.transpose(curT_bank[t % 2][:, 0:P], cur[:, t % 2, :], ident[:, :]).then_inc(curT_psum, 1)
                t = n - 2
                if exists(t):
                    if t == 0:
                        pe.wait_ge(attn_ready, B - 1)
                    pe.wait_ge(hidT_ready, t + 1)
                    if t >= 2:
                        pe.wait_ge(mixed_ready, t - 1)
                    for c in range(HC):
                        last = m.matmul(down_bank[t % 2][:, 0:D], hidT[:, t % 2, c, :],
                                        down[:, bass.ds(starts[2 * t + 1] + c * D, D)], start=(c == 0), stop=(c == HC - 1))
                    last.then_inc(down_psum, 1)

            for n in STEPS:
                step(n)
            pe.wait_ge(mixed_ready, PAIRS)
            attend(EARLY, NT)


_INS = ["L0_attn_x", "L0_attn_WQ", "L0_attn_WK", "L0_attn_WV",
        "L0_ffn_scale", "L0_ffn_centroids", "L0_ffn_up_w", "L0_ffn_down_w"]


def kernel(**inputs):
    import numpy as _np
    import concourse.bacc as _bacc
    from concourse import mybir as _mybir
    from concourse.bass_utils import run_bass_kernel_spmd as _run

    nc = _bacc.Bacc("TRN2", target_bir_lowering=False, num_devices=1)
    arrays, args = {}, []
    for name in _INS:
        a = _np.ascontiguousarray(inputs[name])
        arrays[f"in_{name}_dram"] = a
        args.append(nc.dram_tensor(f"in_{name}_dram", a.shape, _mybir.dt.from_np(a.dtype), kind="ExternalInput").ap())
    batch, seq, dim = inputs["L0_attn_x"].shape
    out = nc.dram_tensor("out_0_dram", (batch, seq, dim), _mybir.dt.float32, kind="ExternalOutput").ap()
    xf_dram = nc.dram_tensor("xf_dram", (batch * seq, dim + 1), _mybir.dt.float32).ap()
    gate_dram = nc.dram_tensor("gate_dram", (batch * seq, dim), _mybir.dt.float32).ap()
    build(nc, *args, out, xf_dram, gate_dram)
    r = _run(nc, [arrays], core_ids=[0])
    return r.results[0]["out_0_dram"]
```

```python
import concourse.bass as bass
from concourse import mybir
from contextlib import ExitStack

F32 = mybir.dt.float32
BF16 = mybir.dt.bfloat16
I32 = mybir.dt.int32
ALU = mybir.AluOpType
ACT = mybir.ActivationFunctionType
AX = mybir.AxisListType

P = 128
MASKED = -1e30
MAX_FLOOR = -1e29
LN_EPS = 1e-5
RMS_EPS = 1e-6


def build(nc, x_in, wq_in, wk_in, wv_in, scale_in, cent_in, up_in, down_in, out, xf_dram, gate_dram):
    B, S, D = x_in.shape
    E = cent_in.shape[0]
    H = down_in.shape[1]
    H2 = 2 * H
    T = B * S
    NT = T // P
    TB = S // P
    HC = H // P
    PAIRS = NT + E - 1
    PAIR_COLS = -(-PAIRS // 4) * 4
    LAG = E - 1
    SCALE = float(D) ** -0.5
    ROW = D + 1
    assert D == P and S == 512 and H2 == 512 and TB == 4

    x_rows = x_in.rearrange("b s d -> (b s) d")
    x_tiles = x_rows.rearrange("(i p) d -> p i d", p=P)
    out_tiles = out.rearrange("b s d -> (b s) d").rearrange("(i p) d -> p i d", p=P)
    xf_tiles = xf_dram.rearrange("(i p) d -> p i d", p=P)
    gate_tiles = gate_dram.rearrange("(i p) d -> p i d", p=P)

    with ExitStack() as ctx:
        def sb(name, shape, dt=F32):
            return ctx.enter_context(nc.sbuf_tensor(name, shape, dt))

        def sem(name):
            return ctx.enter_context(nc.semaphore(name))

        bank = [ctx.enter_context(nc.psum_tensor(f"bank{n}", [P, 512], F32)) for n in range(8)]

        x = sb("x", [P, NT, D])
        wq, wk, wv = sb("wq", [P, D]), sb("wk", [P, D]), sb("wv", [P, D])
        cent = sb("cent", [E, D])
        scale = sb("scale", [P, 1])
        up = sb("up", [P, E * H2])
        down = sb("down", [P, E * HC * D])
        ident = sb("ident", [P, P])
        scale_row = sb("scale_row", [P, D])
        ident_bf = sb("ident_bf", [P, P], BF16)
        causal = sb("causal", [P, P], BF16)
        not_before = sb("not_before", [P, P], BF16)
        ones_bf = sb("ones_bf", [P, P], BF16)
        ones = sb("ones", [P, P])
        lane_no = sb("lane_no", [P, P, NT], BF16)
        tile_no = sb("tile_no", [P, NT, NT], BF16)
        token_no = sb("token_no", [P, 2, NT], BF16)
        expert_no = sb("expert_no", [P, E, NT], BF16)
        carry_on = sb("carry_on", [P, E, NT])
        pair_no = sb("pair_no", [P, PAIR_COLS, E], BF16)
        pair_expert = sb("pair_expert", [P, PAIR_COLS, E], BF16)
        lane_col = sb("lane_col", [P, 1])
        table_test = sb("table_test", [P, 1])
        bn = sb("bn", [P, NT, 6])
        st = {n: sb("st_" + n, [P, NT]) for n in
              ("sum", "dif", "m2", "mean", "dsq", "ssq", "var", "inv", "ratio", "rms2")}
        rad = sb("rad", [P, 2, NT])
        root = sb("root", [P, 2, NT])
        rroot = sb("rroot", [P, 2, NT])
        xn = sb("xn", [P, NT, D])
        xs = sb("xs", [P, NT, D])
        xf = sb("xf", [P, NT, ROW])
        xnT = sb("xnT", [P, T])
        qk = sb("qk", [P, D])
        wvT = sb("wvT", [P, D])
        zT = sb("zT", [P, T])
        pen = sb("pen", [P, 2, S])
        prob = sb("prob", [P, 4, S])
        row_max = sb("row_max", [P, NT])
        neg_max = sb("neg_max", [P, NT])
        row_sum = sb("row_sum", [P, NT])
        row_inv = sb("row_inv", [P, NT])
        probT = sb("probT", [P, 2, TB, S])
        values = sb("values", [P, NT, D])
        attn = sb("attn", [P, NT, D])
        centT_scaled = sb("centT_scaled", [P, E])
        centT_sq = sb("centT_sq", [P, E])
        xs_sq = sb("xs_sq", [P, 4, D])
        xs_norm, nx = sb("xs_norm", [P, NT]), sb("nx", [P, NT])
        rt = {n: sb("rt_" + n, [P, E, NT]) for n in
              ("dot", "norms", "dist", "cum", "base", "full", "pick")}
        nearest, nearest_no = sb("nearest", [P, E, NT], BF16), sb("nearest_no", [P, E, NT], BF16)
        dmin, amin = sb("dmin", [P, NT]), sb("amin", [P, NT], BF16)
        onehot = sb("onehot", [P, E, NT], BF16)
        run = sb("run", [P, E + 1])
        run_i = sb("run_i", [P, 2, E], I32)
        run_tiles, used, pairs_of = (sb(n, [P, E]) for n in ("run_tiles", "used", "pairs_of"))
        pairs_end = sb("pairs_end", [P, E], BF16)
        pairs_start = sb("pairs_start", [P, E])
        place = sb("place", [P, NT], I32)
        place_parts = sb("place_parts", [P, 2, NT], I32)
        place_parts_bf = sb("place_parts_bf", [P, 2, NT], BF16)
        hot_lane = sb("hot_lane", [P, P, NT], BF16)
        hot_tile = sb("hot_tile", [P, NT, NT], BF16)
        hot_val = sb("hot_val", [P, 2, NT, NT], BF16)
        token_of = sb("token_of", [P, NT], I32)
        shift = sb("shift", [P, E], BF16)
        ended = sb("ended", [P, PAIR_COLS, E], BF16)
        expert_f = sb("expert_f", [P, PAIR_COLS], BF16)
        chosen = sb("chosen", [P, PAIR_COLS, E], BF16)
        chosen_shift = sb("chosen_shift", [P, PAIR_COLS, E], BF16)
        pair_shift = sb("pair_shift", [P, PAIR_COLS])
        tile_f = sb("tile_f", [P, PAIR_COLS])
        row_place = sb("row_place", [P, PAIR_COLS])
        passed = sb("passed", [P, PAIR_COLS, E], BF16)
        row_expert = sb("row_expert", [P, PAIR_COLS], BF16)
        pair_mask = sb("pair_mask", [P, PAIR_COLS])
        expert_c = sb("expert_c", [P, PAIR_COLS])
        pair_numbers = sb("pair_numbers", [P, PAIR_COLS * 3], I32)
        rows = sb("rows", [P, NT, ROW])
        rowsT = sb("rowsT", [P, NT, P])
        up_cur = sb("up_cur", [P, 3, H2])
        silu_g = sb("silu_g", [P, 2, HC, P])
        hidT = sb("hidT", [P, 3, HC, P])
        mixed = sb("mixed", [P, NT, D])
        gate = sb("gate", [P, NT, D])
        gate_tok = sb("gate_tok", [P, NT, D])

        x_loaded = [sem(f"x_loaded{b}") for b in range(B)]
        qk_loaded, v_loaded, small_loaded = sem("qk_loaded"), sem("v_loaded"), sem("small_loaded")
        scale_row_loaded = sem("scale_row_loaded")
        up_loaded, down_loaded = sem("up_loaded"), sem("down_loaded")
        tables_loaded = sem("tables_loaded")
        zeroed, ident_made, consts_made = sem("zeroed"), sem("ident_made"), sem("consts_made")
        chain_step, rad_ready, root_ready, stats_ready = (
            sem(n) for n in ("chain_step", "rad_ready", "root_ready", "stats_ready"))
        xn_ready, xf_ready = sem("xn_ready"), sem("xf_ready")
        xf_stored = [sem(f"xf_stored{b}") for b in range(B)]
        weights_psum, weights_ready = sem("weights_psum"), sem("weights_ready")
        norms_psum = sem("norms_psum")
        xnT_psum, xnT_ready = sem("xnT_psum"), sem("xnT_ready")
        xs_ready, xs_norm_ready, xs_norm_ready_2 = sem("xs_ready"), sem("xs_norm_ready"), sem("xs_norm_ready_2")
        zT_psum, zT_ready = sem("zT_psum"), [sem(f"zT_ready{b}") for b in range(B)]
        dist_psum = sem("dist_psum")
        score_psum, pen_ready, masked_ready, max_ready, prob_ready = (
            sem(n) for n in ("score_psum", "pen_ready", "masked_ready", "max_ready", "prob_ready"))
        probT_psum, probT_ready = sem("probT_psum"), sem("probT_ready")
        values_psum, values_ready = sem("values_psum"), sem("values_ready")
        attn_psum, attn_ready, row_inv_ready = sem("attn_psum"), sem("attn_ready"), sem("row_inv_ready")
        onehot_ready, rank_psum = sem("onehot_ready"), sem("rank_psum")
        hot_ready, order_psum, order_ready, pairs_ready = (
            sem(n) for n in ("hot_ready", "order_psum", "order_ready", "pairs_ready"))
        gathered = [sem(f"gathered{t}") for t in range(NT)]
        scattered = sem("scattered")
        mixed_begun = sem("mixed_begun")
        rowsT_psum, rowsT_ready, up_cur_ready, up_psum, silu_ready, hidT_ready = (
            sem(n) for n in ("rowsT_psum", "rowsT_ready", "up_cur_ready", "up_psum", "silu_ready", "hidT_ready"))
        down_psum, mixed_ready, gate_ready = sem("down_psum"), sem("mixed_ready"), sem("gate_ready")
        gates_loaded = [sem(f"gates_loaded{b}") for b in range(B)]
        result_ready = [sem(f"result_ready{b}") for b in range(B + 1)]
        pool_prod_ready, prod_ready, stored = sem("pool_prod_ready"), sem("prod_ready"), sem("stored")

        xnT_bank = bank[0:4]
        zT_bank = [bank[4], bank[5], bank[6], bank[4]]
        route_bank = bank[7]
        dist_ps = route_bank[:, 0:NT * 16].rearrange("p (i c) -> p i c", c=16)
        norm_ps = bank[6][:, 256:256 + E]
        rank_ps = route_bank[:, 0:E * NT]
        count_ps = route_bank[:, E * NT:2 * E * NT]
        order_ps = route_bank[:, 256:256 + 2 * NT]
        score_bank = bank[0:3]
        probT_bank = bank[3:5]
        values_bank = [bank[4], bank[5], bank[5], bank[7]]
        attn_bank = [bank[6], bank[5]]
        last_attn_bank = [bank[5], bank[0], bank[2], bank[1]]
        spare_attn_bank = bank[7]
        up_bank = bank[0:2]
        rowsT_bank = [bank[2], bank[7]]
        down_bank = bank[3:5]

        POOL_BATCHES = 2
        EARLY = 2 * TB

        def width(q):
            return (q + 1) * P

        GATE_LAG = LAG + 3
        STEPS = range(-4, NT + GATE_LAG)
        DRAIN = {-4: EARLY, 0: EARLY + 1, 1: EARLY + 2, 2: EARLY + 3}
        TRANSPOSE = {TB * c - 2: c for c in range(1, NT // TB)}
        assert EARLY % 3 == 2
        CHUNK = 4
        assert PAIRS <= PAIR_COLS and PAIR_COLS % CHUNK == 0 and CHUNK == TB

        def exists(p):
            return 0 <= p < PAIRS

        def load_numbers(eng, table, name, c, per_pair, most):
            regs = [eng.alloc_register(f"{name}{c * CHUNK + i // per_pair}_{i % per_pair}")
                    for i in range(CHUNK * per_pair)]
            eng.load(regs, table[0:1, c * CHUNK * per_pair:(c + 1) * CHUNK * per_pair])
            return [eng.snap(r, donate=True, min_val=0, max_val=most[i % per_pair]) for i, r in enumerate(regs)]

        def tile_at(t, tile):
            return t[:, bass.ds(tile, 1), :].rearrange("p a d -> p (a d)")

        block = ctx.enter_context(nc.Block())

        @block.sync
        def _(sp):
            for b in range(B):
                sp.dma_start(x[:, b * TB:(b + 1) * TB, :], x_tiles[:, b * TB:(b + 1) * TB, :]
                             ).then_inc(x_loaded[b], 16)
            sp.dma_start(wq[:, :], wq_in).then_inc(qk_loaded, 16)
            sp.dma_start(wk[:, :], wk_in).then_inc(qk_loaded, 16)
            sp.dma_start(cent[:, :], cent_in).then_inc(small_loaded, 16)
            sp.dma_start(scale[:, :], scale_in.rearrange("(p a) -> p a", a=1)).then_inc(small_loaded, 16)
            sp.dma_start(wv[:, :], wv_in).then_inc(v_loaded, 16)
            sp.dma_start(scale_row[:, :], scale_in.rearrange("(a d) -> a d", a=1).broadcast_to([P, D])
                         ).then_inc(scale_row_loaded, 16)
            sp.dma_start(up[:, :].rearrange("p (e n) -> p e n", e=E), up_in.rearrange("e d h -> d e h")
                         ).then_inc(up_loaded, 16)
            sp.dma_start(down[:, :].rearrange("p (e c n) -> p e c n", e=E, c=HC),
                         down_in.rearrange("e (c p) d -> p e c d", p=P)).then_inc(down_loaded, 16)
            for b in range(B):
                sp.wait_ge(xf_ready, (b + 1) * (TB + 1))
                sp.dma_start(xf_tiles[:, b * TB:(b + 1) * TB, :], xf[:, b * TB:(b + 1) * TB, :]
                             ).then_inc(xf_stored[b], 16)
            sp.wait_ge(scattered, 16 * NT)
            for b in range(B):
                sp.dma_start(gate_tok[:, b * TB:(b + 1) * TB, :], gate_tiles[:, b * TB:(b + 1) * TB, :]
                             ).then_inc(gates_loaded[b], 16)
            parts = [(b * TB, (b + 1) * TB) for b in range(B - 1)] + [(NT - TB, NT - 1), (NT - 1, NT)]
            for b in [0, 2, 1, 3, 4]:
                first, end = parts[b]
                sp.wait_ge(result_ready[b], {B - 2: 2, B - 1: TB - 1}.get(b, 1))
                sp.dma_start(out_tiles[:, first:end, :], gate_tok[:, first:end, :]).then_inc(stored, 16)
            sp.wait_ge(stored, 16 * (B + 1))

        @block.gpsimd
        def _(pool):
            g = nc.gpsimd
            g.memset(ident[:, :], 0.0).then_inc(zeroed, 1)
            g.memset(ident_bf[:, :], 0.0).then_inc(zeroed, 1)
            g.memset(causal[:, :], 0.0).then_inc(zeroed, 1)
            g.memset(not_before[:, :], -1.0).then_inc(zeroed, 1)
            g.memset(ones[:, :], 1.0).then_inc(zeroed, 1)
            pool.wait_ge(zeroed, 5)
            g.affine_select(out=ident[:, :], in_=ident[:, :], compare_op=ALU.not_equal, fill=1.0, base=0,
                            pattern=[[-1, P]], channel_multiplier=1).then_inc(ident_made, 1)
            g.affine_select(out=ident_bf[:, :], in_=ident_bf[:, :], compare_op=ALU.not_equal, fill=1.0,
                            base=0, pattern=[[-1, P]], channel_multiplier=1).then_inc(ident_made, 1)
            g.affine_select(out=causal[:, :], in_=causal[:, :], compare_op=ALU.is_ge, fill=MASKED, base=0,
                            pattern=[[-1, P]], channel_multiplier=1).then_inc(ident_made, 1)
            g.affine_select(out=not_before[:, :], in_=not_before[:, :], compare_op=ALU.is_ge, fill=0.0, base=0,
                            pattern=[[-1, P]], channel_multiplier=1).then_inc(consts_made, 1)
            g.memset(ones_bf[:, :], 1.0).then_inc(consts_made, 1)
            g.memset(carry_on[:, :, 1:NT], 1.0).then_inc(consts_made, 1)
            g.memset(carry_on[:, :, 0:1], 0.0).then_inc(consts_made, 1)
            g.memset(run[:, 0:1], 0.0).then_inc(consts_made, 1)

            def count(dst, pattern, base, lanes):
                g.iota(dst, pattern=pattern, base=base, channel_multiplier=lanes,
                       allow_small_or_imprecise_dtypes=True).then_inc(consts_made, 1)

            count(expert_no[:, :, :], [[1, E], [0, NT]], -E, 0)
            count(lane_no[:, :, :], [[1, P], [0, NT]], 0, 0)
            count(tile_no[:, :, :], [[1, NT], [0, NT]], 0, 0)
            count(token_no[:, 0, :], [[P, NT]], 0, 0)
            count(token_no[:, 1, :], [[0, NT]], 0, 1)
            count(pair_no[:, :, :], [[1, PAIR_COLS], [0, E]], 0, 0)
            count(pair_expert[:, :, :], [[0, PAIR_COLS], [1, E]], 0, 0)
            count(lane_col[:, :], [[0, 1]], 0, 1)
            pool.wait_ge(scale_row_loaded, 16)
            for b in range(B):
                tiles = slice(b * TB, (b + 1) * TB)
                pool.wait_ge(xn_ready, (b + 1) * TB)
                g.tensor_tensor(xs[:, tiles, :], xn[:, tiles, :],
                                scale_row[:, :].unsqueeze(1).broadcast_to([P, TB, D]), ALU.mult
                                ).then_inc(xs_ready, 1)
            pool.wait_ge(stats_ready, 1)
            for b in range(B):
                for i in range(b * TB, (b + 1) * TB):
                    g.tensor_scalar(xf[:, i, 0:D], xn[:, i, :], rroot[:, 1, i:i + 1], 1.0, ALU.mult, ALU.mult
                                    ).then_inc(xf_ready, 1)
                g.tensor_copy(xf[:, b * TB:(b + 1) * TB, D:ROW],
                              root[:, 1, b * TB:(b + 1) * TB].unsqueeze(2)).then_inc(xf_ready, 1)
            for b in range(B):
                pool.wait_ge(xf_stored[b], 16)
            pool.wait_ge(order_ready, 1)
            AHEAD = 3
            for t in range(NT + AHEAD):
                if t < NT:
                    g.indirect_dma_start(rows[:, t, :], None, xf_dram,
                                         bass.IndirectOffsetOnAxis(token_of[:, t:t + 1], 0)
                                         ).then_inc(gathered[t], 16)
                if t >= AHEAD:
                    u = t - AHEAD
                    pool.wait_ge(gathered[u], 16)
                    g.tensor_scalar(mixed[:, u, :], rows[:, u, 0:D], rows[:, u, D:ROW], 1.0, ALU.mult, ALU.mult
                                    ).then_inc(mixed_begun, 1)
            for t in range(NT):
                pool.wait_ge(gate_ready, t + 1)
                g.indirect_dma_start(gate_dram, bass.IndirectOffsetOnAxis(token_of[:, t:t + 1], 0),
                                     gate[:, t, :], None).then_inc(scattered, 16)
            for b in range(POOL_BATCHES):
                tiles = slice(b * TB, (b + 1) * TB)
                pool.wait_ge(attn_ready, b + 1)
                pool.wait_ge(gates_loaded[b], 16)
                g.tensor_tensor(gate_tok[:, tiles, :], attn[:, tiles, :], gate_tok[:, tiles, :], ALU.mult
                                ).then_inc(pool_prod_ready, 1)
                pool.wait_ge(pool_prod_ready, b + 1)
                g.tensor_tensor(gate_tok[:, tiles, :], gate_tok[:, tiles, :], x[:, tiles, :], ALU.add
                                ).then_inc(result_ready[b], 1)

        @block.scalar
        def _(act):
            a = nc.scalar
            def load_table(func):
                a.activation(table_test[:, :], ones[:, 0:1], func).then_inc(tables_loaded, 1)

            def copy_z(b):
                act.wait_ge(zT_psum, b + 1)
                a.activation(zT[:, b * S:(b + 1) * S], zT_bank[b][:, :], ACT.Copy).then_inc(zT_ready[b], 1)

            def copy_probT(n):
                b, q = divmod(n, TB)
                act.wait_ge(probT_psum, n + 1)
                if b >= 2:
                    act.wait_ge(attn_psum, n - 2 * TB + 1)
                a.activation(probT[:, b % 2, 0:q + 1, q * P:(q + 1) * P],
                                     probT_bank[n % 2][:, 0:width(q)].rearrange("p (j c) -> p j c", c=P),
                                     ACT.Copy).then_inc(probT_ready, 1)

            def copy_values(b):
                act.wait_ge(values_psum, b + 1)
                a.activation(values[:, b * TB:(b + 1) * TB, :], values_bank[b][:, :].rearrange("p (i d) -> p i d", d=D),
                             ACT.Copy).then_inc(values_ready, 1)

            act.wait_ge(zeroed, 5)
            load_table(ACT.Sqrt)

            def square_roots(k, row, tiles):
                act.wait_ge(rad_ready, k)
                a.activation(root[:, row, tiles], rad[:, row, tiles], ACT.Sqrt).then_inc(root_ready, 1)

            square_roots(1, 0, slice(0, NT // 2))
            act.wait_ge(weights_psum, 3)
            act.wait_ge(small_loaded, 32)
            a.activation(centT_scaled[:, :], bank[6][:, 0:E], ACT.Identity, bias=0.0,
                         scale=scale[:, 0:1]).then_inc(weights_ready, 1)
            a.activation(centT_sq[:, :], bank[6][:, 0:E], ACT.Square).then_inc(weights_ready, 1)
            a.activation(qk[:, :], bank[4][:, 0:D], ACT.Copy).then_inc(weights_ready, 1)
            a.activation(wvT[:, :], bank[5][:, 0:D], ACT.Copy).then_inc(weights_ready, 1)

            def copy_xT(b):
                act.wait_ge(xnT_psum, b + 1)
                a.activation(xnT[:, b * S:(b + 1) * S], xnT_bank[b][:, :], ACT.Copy).then_inc(xnT_ready, 1)

            def norms(b):
                act.wait_ge(xs_ready, b + 1)
                for i in range(b * TB, (b + 1) * TB):
                    if i >= 2:
                        act.wait_ge(xs_norm_ready, i - 1)
                    a.activation(xs_sq[:, i % 2, :], xs[:, i, :], ACT.Square, accum_out=xs_norm[:, i:i + 1]
                                 ).then_inc(xs_norm_ready, 1)

            copy_xT(0)
            square_roots(2, 0, slice(NT // 2, NT))
            copy_xT(1)
            square_roots(3, 1, slice(0, NT))
            norms(0)
            copy_xT(2)
            copy_xT(3)
            norms(1)
            copy_z(0)
            act.wait_ge(tables_loaded, 1)
            load_table(ACT.Exp)

            def exponentiate(n):
                w = width(n % TB)
                act.wait_ge(max_ready, n + 1)
                a.activation(prob[:, n % 4, 0:w], prob[:, n % 4, 0:w], ACT.Exp, bias=neg_max[:, n:n + 1],
                             scale=SCALE, accum_out=row_sum[:, n:n + 1]).then_inc(prob_ready, 1)

            def attend(n, first, end):
                if first <= n - 3 < end:
                    copy_probT(n - 3)
                if n == 4:
                    copy_values(2)
                if first <= n - 1 < end:
                    exponentiate(n - 1)

            def copy_rowsT(c):
                act.wait_ge(rowsT_psum, c + 1)
                a.activation(rowsT[:, c * TB:(c + 1) * TB, :], rowsT_bank[c % 2][:, :].rearrange("p (i c) -> p i c", c=P),
                             ACT.Identity, bias=0.0, scale=scale[:, 0:1]).then_inc(rowsT_ready, 1)

            for n in range(EARLY):
                if n == 1:
                    copy_z(1)
                if n == 3:
                    copy_values(0)
                    copy_values(1)
                    copy_z(2)
                    copy_z(3)
                attend(n, 0, EARLY)
                if n == EARLY - 1:
                    copy_rowsT(0)
                if n == EARLY - 1:
                    copy_values(3)
            act.wait_ge(tables_loaded, 2)

            def step(n):
                if n == 0:
                    load_table(ACT.Silu)
                if n in DRAIN and n >= 0:
                    attend(DRAIN[n], 0, EARLY)
                if n in TRANSPOSE:
                    copy_rowsT(TRANSPOSE[n])
                if n in DRAIN and n < 0:
                    attend(DRAIN[n], 0, EARLY)
                t = n
                if exists(t):
                    act.wait_ge(up_psum, t + 1)
                    if t >= 2:
                        act.wait_ge(hidT_ready, t - 1)
                    a.activation(silu_g[:, t % 2, :, :], up_bank[t % 2][:, H:H2].rearrange("p (c i) -> p c i", c=HC),
                                 ACT.Silu).then_inc(silu_ready, 1)
                t = n - GATE_LAG
                if 0 <= t < NT:
                    act.wait_ge(mixed_ready, t + LAG + 1)
                    a.activation(gate[:, t, :], mixed[:, t, :], ACT.Silu).then_inc(gate_ready, 1)

            for n in STEPS:
                step(n)
            act.wait_ge(tables_loaded, 3)
            load_table(ACT.Exp)
            for n in range(EARLY, NT + 4):
                attend(n, EARLY, NT)

        @block.vector
        def _(dve):
            v = nc.vector
            steps = [0]

            def link(ins, meanwhile=None):
                steps[0] += 1
                done = steps[0]
                ins.then_inc(chain_step, 1)
                if meanwhile:
                    meanwhile()
                dve.wait_ge(chain_step, done)

            aside_done = [0]

            def aside(issue):
                if aside_done[0]:
                    dve.wait_ge(chain_step, aside_done[0])
                steps[0] += 1
                aside_done[0] = steps[0]
                issue().then_inc(chain_step, 1)

            def moments(i):
                if i % TB == 0:
                    dve.wait_ge(x_loaded[i // TB], 16)
                return v.bn_stats(bn[:, i, :], x[:, i, :])

            s_ = {n: t[:, :] for n, t in st.items()}

            def deviations(half, meanwhile):
                tiles = slice(half * NT // 2, (half + 1) * NT // 2)
                h = {n: t[:, tiles] for n, t in st.items()}
                mean_e, m2_e, mean_o, m2_o = (bn[:, tiles, c] for c in (1, 2, 4, 5))
                v.tensor_tensor(h["sum"], mean_e, mean_o, ALU.add)
                v.tensor_tensor(h["m2"], m2_e, m2_o, ALU.add)
                link(v.tensor_tensor(h["dif"], mean_e, mean_o, ALU.subtract), lambda: meanwhile[0]())
                link(v.tensor_tensor(h["dsq"], h["dif"], h["dif"], ALU.mult), lambda: meanwhile[1]())
                link(v.scalar_tensor_tensor(out=h["ssq"], in0=h["dsq"], scalar=D / 4, in1=h["m2"],
                                            op0=ALU.mult, op1=ALU.add), lambda: meanwhile[2]())
                v.tensor_scalar(rad[:, 0, tiles], h["ssq"], 1.0 / D, LN_EPS, ALU.mult, ALU.add).then_inc(rad_ready, 1)
                v.tensor_scalar(h["mean"], h["sum"], 0.5, None, ALU.mult)

            def invert_root(half):
                tiles = slice(half * NT // 2, (half + 1) * NT // 2)
                dve.wait_ge(root_ready, half + 1)
                return v.reciprocal(rroot[:, 0, tiles], root[:, 0, tiles])

            def normalise(i):
                v.tensor_scalar(xn[:, i, :], x[:, i, :], st["mean"][:, i:i + 1], rroot[:, 0, i:i + 1],
                                ALU.subtract, ALU.mult).then_inc(xn_ready, 1)

            for i in range(NT // 2):
                last = moments(i)
            link(last)
            deviations(0, [lambda: moments(8), lambda: moments(9), lambda: moments(10)])
            moments(11)
            moments(12)
            link(invert_root(0), lambda: moments(13))
            for i in range(4):
                normalise(i)
            moments(14)
            link(moments(15), lambda: normalise(4))
            deviations(1, [lambda: normalise(5), lambda: normalise(6), lambda: normalise(7)])
            link(v.tensor_scalar(s_["var"], s_["ssq"], 1.0 / D, None, ALU.mult))
            link(v.reciprocal(s_["inv"], rad[:, 0, :]))
            link(invert_root(1))
            link(v.tensor_tensor(s_["ratio"], s_["var"], s_["inv"], ALU.mult), lambda: normalise(8))
            v.tensor_scalar(rad[:, 1, :], s_["ratio"], RMS_EPS, None, ALU.add).then_inc(rad_ready, 1)
            for i in range(9, NT):
                normalise(i)
            dve.wait_ge(root_ready, 3)
            link(v.reciprocal(rroot[:, 1, :], root[:, 1, :]))
            v.tensor_tensor(st["rms2"][:, :], rroot[:, 1, :], rroot[:, 1, :], ALU.mult).then_inc(stats_ready, 1)

            def over_tiles(ap):
                return ap.unsqueeze(2).broadcast_to([P, E, NT])

            def over_experts(ap):
                return ap.unsqueeze(1).broadcast_to([P, E, NT])

            def norms(b):
                dve.wait_ge(xs_ready, b + 1)
                for i in range(b * TB, (b + 1) * TB):
                    if i >= 2 * TB + 2:
                        dve.wait_ge(xs_norm_ready_2, i - 2 * TB - 1)
                    v.tensor_tensor_reduce(xs_sq[:, 2 + i % 2, :], xs[:, i, :], xs[:, i, :], 1.0, 0.0, ALU.mult, ALU.add,
                                           xs_norm[:, i:i + 1]).then_inc(xs_norm_ready_2, 1)

            def choose_experts():
                dve.wait_ge(consts_made, 13)
                dve.wait_ge(stats_ready, 1)
                dve.wait_ge(dist_psum, 1)
                v.scalar_tensor_tensor(out=rt["dot"][:, :, :], in0=dist_ps[:, :, 0:E].rearrange("p i e -> p e i"),
                                       scalar=-2.0, in1=over_experts(rroot[:, 1, :]), op0=ALU.mult, op1=ALU.mult)
                dve.wait_ge(xs_norm_ready, 2 * TB)
                dve.wait_ge(xs_norm_ready_2, 2 * TB)
                link(v.tensor_tensor(nx[:, :], xs_norm[:, :], st["rms2"][:, :], ALU.mult))
                dve.wait_ge(norms_psum, 1)
                link(v.tensor_tensor(rt["norms"][:, :, :], over_experts(nx[:, :]), over_tiles(norm_ps), ALU.add))
                link(v.tensor_tensor(rt["dist"][:, :, :], rt["norms"][:, :, :], rt["dot"][:, :, :], ALU.add))
                link(v.tensor_reduce(dmin[:, :], rt["dist"][:, :, :].rearrange("p e i -> p i e"), AX.X, ALU.min),
                     lambda: mask_zeros(0))
                link(v.tensor_tensor(nearest[:, :, :], rt["dist"][:, :, :], over_experts(dmin[:, :]), ALU.is_equal),
                     lambda: find_max(0))
                link(v.tensor_tensor(nearest_no[:, :, :], nearest[:, :, :], expert_no[:, :, :], ALU.mult))
                with nc.allow_low_precision(reason="experts are whole numbers below 2^8"):
                    link(v.tensor_reduce(amin[:, :], nearest_no[:, :, :].rearrange("p e i -> p i e"), AX.X, ALU.min))
                v.tensor_tensor(onehot[:, :, :], expert_no[:, :, :], over_experts(amin[:, :]), ALU.is_equal
                                ).then_inc(onehot_ready, 1)

            def hot_lanes():
                v.tensor_tensor(hot_lane[:, :, :], place_parts_bf[:, 0, :].unsqueeze(1).broadcast_to([P, P, NT]),
                                lane_no[:, :, :], ALU.is_equal).then_inc(hot_ready, 1)

            def place_tokens():
                flat = "p e i -> p (e i)"
                dve.wait_ge(rank_psum, 1)
                link(v.tensor_tensor_scan(rt["cum"][:, :, :].rearrange(flat), carry_on[:, :, :].rearrange(flat),
                                          count_ps, 0.0, ALU.mult, ALU.add), lambda: negate_max(1))
                link(v.tensor_tensor_scan(run[:, 1:E + 1], ones[:, 0:E], rt["cum"][:, :, NT - 1], 0.0,
                                          ALU.mult, ALU.add))
                link(v.tensor_tensor(rt["base"][:, :, :], over_tiles(run[:, 0:E]), rt["cum"][:, :, :], ALU.add), run_bounds)
                link(v.tensor_tensor(rt["full"][:, :, :].rearrange(flat), rt["base"][:, :, :].rearrange(flat),
                                     rank_ps, ALU.add), run_tile_bounds)
                link(v.tensor_tensor(rt["pick"][:, :, :], rt["full"][:, :, :], onehot[:, :, :], ALU.mult), count_tiles)
                with nc.allow_low_precision(reason="places are whole numbers below 2^24"):
                    link(v.tensor_reduce(place[:, :], rt["pick"][:, :, :].rearrange("p e i -> p i e"), AX.X, ALU.add),
                         count_pairs)
                v.tensor_scalar(place_parts[:, 1, :], place[:, :], 7, None, ALU.logical_shift_right)
                link(v.tensor_scalar(place_parts[:, 0, :], place[:, :], P - 1, None, ALU.bitwise_and), sum_pairs)
                link(v.tensor_copy(place_parts_bf[:, :, :], place_parts[:, :, :]), begin_pairs)
                shift_tiles()
                link(v.tensor_tensor(hot_tile[:, :, :], place_parts_bf[:, 1, :].unsqueeze(1).broadcast_to([P, NT, NT]),
                                     tile_no[:, :, :], ALU.is_equal), hot_lanes)
                v.tensor_tensor(hot_val[:, :, :, :], hot_tile[:, :, :].unsqueeze(1).broadcast_to([P, 2, NT, NT]),
                                token_no[:, :, :].unsqueeze(2).broadcast_to([P, 2, NT, NT]), ALU.mult
                                ).then_inc(hot_ready, 1)

            def read_order():
                dve.wait_ge(order_psum, 1)
                with nc.allow_low_precision(reason="tokens are whole numbers below 2^24"):
                    v.tensor_reduce(token_of[:, :], order_ps.rearrange("p (c a) -> p a c", c=2), AX.X, ALU.add
                                    ).then_inc(order_ready, 1)

            start, end = run[:, 0:E], run[:, 1:E + 1]

            def run_bounds():
                v.tensor_copy(run_i[:, 0, :], start)
                v.tensor_tensor(used[:, :], end, start, ALU.is_gt)
                aside(lambda: v.tensor_scalar(run_i[:, 1, :], end, float(P - 1), None, ALU.add))

            def run_tile_bounds():
                aside(lambda: v.tensor_scalar(run_i[:, :, :], run_i[:, :, :], 7, None, ALU.logical_shift_right))

            def count_tiles():
                aside(lambda: v.tensor_tensor(run_tiles[:, :], run_i[:, 1, :], run_i[:, 0, :], ALU.subtract))

            def count_pairs():
                aside(lambda: v.tensor_tensor(pairs_of[:, :], run_tiles[:, :], used[:, :], ALU.mult))

            def sum_pairs():
                aside(lambda: v.tensor_tensor_scan(pairs_end[:, :], ones[:, 0:E], pairs_of[:, :], 0.0, ALU.mult, ALU.add))

            def begin_pairs():
                aside(lambda: v.tensor_tensor(pairs_start[:, :], pairs_end[:, :], pairs_of[:, :], ALU.subtract))

            def shift_tiles():
                aside(lambda: v.tensor_tensor(shift[:, :], run_i[:, 0, :], pairs_start[:, :], ALU.subtract))

            def list_pairs(n):
                shape = [P, PAIR_COLS, E]
                dve.wait_ge(chain_step, aside_done[0])
                link(v.tensor_tensor(ended[:, :, :], pairs_end[:, :].unsqueeze(1).broadcast_to(shape),
                                     pair_no[:, :, :], ALU.is_le), lambda: mask_zeros(n))
                with nc.allow_low_precision(reason="experts and tiles are whole numbers below 2^8"):
                    link(v.tensor_reduce(expert_f[:, :], ended[:, :, :], AX.X, ALU.add), lambda: negate_max(n - 1))
                v.tensor_scalar(expert_c[:, :], expert_f[:, :], float(E - 1), None, ALU.min)
                link(v.tensor_tensor(chosen[:, :, :], expert_f[:, :].unsqueeze(2).broadcast_to(shape),
                                     pair_expert[:, :, :], ALU.is_equal), lambda: find_max(n))
                link(v.tensor_tensor(chosen_shift[:, :, :], chosen[:, :, :], shift[:, :].unsqueeze(1).broadcast_to(shape),
                                     ALU.mult), lambda: mask_zeros(n + 1))
                link(v.tensor_reduce(pair_shift[:, :], chosen_shift[:, :, :], AX.X, ALU.add), lambda: negate_max(n))

            def place_pairs(n):
                link(v.tensor_tensor(tile_f[:, :], pair_shift[:, :], pair_no[:, :, 0], ALU.add), lambda: find_max(n))
                link(v.tensor_scalar(tile_f[:, :], tile_f[:, :], float(NT - 1), None, ALU.min))
                numbers = pair_numbers[:, :].rearrange("p (n k) -> p n k", k=3)
                v.tensor_copy(numbers[:, :, 0], tile_f[:, :])
                v.tensor_scalar(numbers[:, :, 1], expert_c[:, :], float(H2), None, ALU.mult)
                v.tensor_scalar(numbers[:, :, 2], expert_c[:, :], float(H), None, ALU.mult)
                v.engine_nop().then_inc(pairs_ready, 1)

            def mask_pairs():
                shape = [P, PAIR_COLS, E]
                link(v.tensor_scalar(row_place[:, :], tile_f[:, :], float(P), lane_col[:, 0:1], ALU.mult, ALU.add))
                link(v.tensor_tensor(passed[:, :, :], row_place[:, :].unsqueeze(2).broadcast_to(shape),
                                     run[:, 1:E + 1].unsqueeze(1).broadcast_to(shape), ALU.is_ge))
                with nc.allow_low_precision(reason="experts are whole numbers below 2^8"):
                    link(v.tensor_reduce(row_expert[:, :], passed[:, :, :], AX.X, ALU.add))
                link(v.tensor_tensor(pair_mask[:, :], row_expert[:, :], expert_f[:, :], ALU.is_equal))

            def mask_zeros(n):
                w = width(n % TB)
                dve.wait_ge(score_psum, n + 1)
                if n >= 2:
                    dve.wait_ge(masked_ready, n - 1)
                v.tensor_scalar(pen[:, n % 2, 0:w], score_bank[n % 3][:, 0:w], 0.0, MASKED,
                                ALU.is_equal, ALU.mult).then_inc(pen_ready, 1)

            def find_max(n):
                w = width(n % TB)
                dve.wait_ge(pen_ready, n + 1)
                if n >= 4:
                    dve.wait_ge(probT_psum, n - 3)
                v.tensor_tensor_reduce(prob[:, n % 4, 0:w], score_bank[n % 3][:, 0:w], pen[:, n % 2, 0:w],
                                       1.0, MASKED, ALU.add, ALU.max, row_max[:, n:n + 1]
                                       ).then_inc(masked_ready, 1)

            def negate_max(n):
                dve.wait_ge(masked_ready, n + 1)
                v.tensor_scalar(neg_max[:, n:n + 1], row_max[:, n:n + 1], MAX_FLOOR, -SCALE,
                                ALU.max, ALU.mult).then_inc(max_ready, 1)

            def finish_attention(b):
                tiles = slice(b * TB, (b + 1) * TB)
                dve.wait_ge(prob_ready, (b + 1) * TB)
                v.reciprocal(row_inv[:, tiles], row_sum[:, tiles]).then_inc(row_inv_ready, 1)
                dve.wait_ge(row_inv_ready, b + 1)
                dve.wait_ge(attn_psum, (b + 1) * TB)
                v.tensor_tensor(attn[:, tiles, :], attn_bank[b % 2][:, :].rearrange("p (i d) -> p i d", d=D),
                                row_inv[:, tiles].unsqueeze(2).broadcast_to([P, TB, D]), ALU.mult
                                ).then_inc(attn_ready, 1)

            def finish_most(b):
                first, end = b * TB, (b + 1) * TB - 1
                tiles = slice(first, end)
                dve.wait_ge(prob_ready, end)
                link(v.reciprocal(row_inv[:, tiles], row_sum[:, tiles]))
                dve.wait_ge(attn_psum, end)
                link(v.tensor_tensor(attn[:, tiles, :], attn_bank[b % 2][:, 0:(TB - 1) * D].rearrange("p (i d) -> p i d", d=D),
                                     row_inv[:, tiles].unsqueeze(2).broadcast_to([P, TB - 1, D]), ALU.mult))
                dve.wait_ge(gates_loaded[b], 16)
                link(v.tensor_tensor(gate_tok[:, tiles, :], attn[:, tiles, :], gate_tok[:, tiles, :], ALU.mult))
                v.tensor_tensor(gate_tok[:, tiles, :], gate_tok[:, tiles, :], x[:, tiles, :], ALU.add
                                ).then_inc(result_ready[b], 1)

            def attend(n, first, end):
                if n < end:
                    mask_zeros(n)
                if first < n <= end:
                    negate_max(n - 1)
                if n < end:
                    find_max(n)
                if n == NT:
                    finish_most(B - 2)

            norms(2)
            norms(3)
            choose_experts()
            negate_max(0)
            mask_zeros(1)
            find_max(1)
            place_tokens()
            mask_zeros(2)
            find_max(2)
            read_order()
            negate_max(2)
            mask_zeros(3)
            find_max(3)
            attend(4, 0, EARLY)
            list_pairs(5)
            place_pairs(6)
            up_starts, tiles = [], []

            def load_pairs(c):
                if c == 0:
                    dve.wait_ge(pairs_ready, 1)
                numbers = load_numbers(dve, pair_numbers, "number", c, 3, [NT - 1, (E - 1) * H2, (E - 1) * H])
                tiles.extend(numbers[0::3])
                up_starts.extend(numbers[1::3])

            def copy_up(t):
                if t >= 3:
                    dve.wait_ge(up_psum, t - 2)
                else:
                    dve.wait_ge(up_loaded, 16)
                v.tensor_copy(up_cur[:, t % 3, :], up[:, bass.ds(up_starts[t], H2)]).then_inc(up_cur_ready, 1)

            mask_zeros(EARLY - 1)
            negate_max(EARLY - 2)
            find_max(EARLY - 1)
            load_pairs(0)
            copy_up(0)
            negate_max(EARLY - 1)

            def step(n):
                t = n + 2
                if exists(t) and t > 0:
                    if t % CHUNK == 0:
                        load_pairs(t // CHUNK)
                    copy_up(t)
                t = n
                if exists(t):
                    dve.wait_ge(silu_ready, t + 1)
                    if t >= 3:
                        dve.wait_ge(down_psum, t - 2)
                    v.tensor_tensor(hidT[:, t % 3, :, :], up_bank[t % 2][:, 0:H].rearrange("p (c i) -> p c i", c=HC),
                                    silu_g[:, t % 2, :, :], ALU.mult).then_inc(hidT_ready, 1)
                t = n - 2
                if exists(t):
                    dve.wait_ge(down_psum, t + 1)
                    dve.wait_ge(mixed_begun, min(t, NT - 1) + 1)
                    if t >= 1:
                        dve.wait_ge(mixed_ready, t)
                    v.scalar_tensor_tensor(out=tile_at(mixed, tiles[t]), in0=down_bank[t % 2][:, 0:D],
                                           scalar=pair_mask[:, t:t + 1], in1=tile_at(mixed, tiles[t]),
                                           op0=ALU.mult, op1=ALU.add).then_inc(mixed_ready, 1)
                if n == -1:
                    finish_attention(0)
                if n == 0:
                    mask_pairs()
                if n == 3:
                    finish_attention(1)

            for n in STEPS:
                step(n)
            for n in range(EARLY, NT + 1):
                attend(n, EARLY, NT)

            dve.wait_ge(prob_ready, NT)
            link(v.reciprocal(row_inv[:, NT - TB - 1:NT], row_sum[:, NT - TB - 1:NT]))
            dve.wait_ge(gates_loaded[B - 1], 16)

            def multiply(n):
                where = spare_attn_bank if n < NT - TB else last_attn_bank[n % TB]
                dve.wait_ge(attn_psum, n + 1)
                v.scalar_tensor_tensor(out=gate_tok[:, n, :], in0=where[:, 0:D], scalar=row_inv[:, n:n + 1],
                                       in1=gate_tok[:, n, :], op0=ALU.mult, op1=ALU.mult).then_inc(prod_ready, 1)

            first = NT - TB - 1
            multiply(first)
            for n in range(first, NT):
                if n + 1 < NT:
                    multiply(n + 1)
                dve.wait_ge(prod_ready, n - first + 1)
                done = result_ready[B if n == NT - 1 else n // TB]
                v.tensor_tensor(gate_tok[:, n, :], gate_tok[:, n, :], x[:, n, :], ALU.add).then_inc(done, 1)

        @block.tensor
        def _(pe):
            m = nc.tensor
            def keep_busy(turns, free_bank):
                with pe.Fori(0, turns) as _:
                    for _ in range(8):
                        m.matmul(free_bank[:, 0:P], ident_bf[:, :], ident_bf[:, :], start=True, stop=True)

            pe.wait_ge(ident_made, 3)
            keep_busy(4, bank[7])
            pe.wait_ge(small_loaded, 32)
            m.transpose(bank[6][:, 0:E], cent[:, :], ident[0:E, 0:E]).then_inc(weights_psum, 1)
            pe.wait_ge(qk_loaded, 32)
            m.matmul(bank[4][:, 0:D], wq[:, :], wk[:, :], start=True, stop=True).then_inc(weights_psum, 1)
            pe.wait_ge(v_loaded, 16)
            m.transpose(bank[5][:, 0:D], wv[:, :], ident[:, :]).then_inc(weights_psum, 1)
            keep_busy(1, bank[7])

            def transpose_tokens(b):
                for i in range(TB):
                    pe.wait_ge(xn_ready, b * TB + i + 1)
                    last = m.transpose(xnT_bank[b][:, i * P:(i + 1) * P], xn[:, b * TB + i, :], ident[:, :])
                last.then_inc(xnT_psum, 1)

            def project_queries(b):
                pe.wait_ge(xnT_ready, b + 1)
                if b == 0:
                    pe.wait_ge(weights_ready, 4)
                m.matmul(zT_bank[b][:, :], qk[:, :], xnT[:, b * S:(b + 1) * S], start=True, stop=True
                         ).then_inc(zT_psum, 1)

            def distances(b):
                pe.wait_ge(xnT_ready, b + 1)
                if b == 0:
                    pe.wait_ge(weights_ready, 4)
                for i in range(b * TB, (b + 1) * TB):
                    last = m.matmul(dist_ps[:, i, 0:E], xnT[:, i * P:(i + 1) * P], centT_scaled[:, :], start=True, stop=True)
                if b == B - 1:
                    last.then_inc(dist_psum, 1)

            transpose_tokens(0)
            transpose_tokens(1)
            distances(0)
            m.matmul(norm_ps, ones[:, :], centT_sq[:, :], start=True, stop=True).then_inc(norms_psum, 1)
            project_queries(0)
            transpose_tokens(2)
            distances(1)
            transpose_tokens(3)
            distances(2)
            distances(3)
            project_queries(1)

            def rank_tokens():
                pe.wait_ge(onehot_ready, 1)
                hot = onehot[:, :, :].rearrange("p e i -> p (e i)")
                m.matmul(rank_ps, not_before[:, :], hot, start=True, stop=True)
                m.matmul(count_ps, ones_bf[:, :], hot, start=True, stop=True).then_inc(rank_psum, 1)

            def invert_order():
                pe.wait_ge(hot_ready, 2)
                for i in range(NT):
                    last = m.matmul(order_ps, hot_lane[:, :, i], hot_val[:, :, :, i].rearrange("p c a -> p (c a)"),
                                    start=(i == 0), stop=(i == NT - 1))
                last.then_inc(order_psum, 1)

            def scores(n):
                b, q = divmod(n, TB)
                w = width(q)
                if n >= 3:
                    pe.wait_ge(masked_ready, n - 2)
                if q == 0:
                    pe.wait_ge(zT_ready[b], 1)
                m.matmul(score_bank[n % 3][:, 0:w], zT[:, n * P:(n + 1) * P], xnT[:, b * S:b * S + w],
                         start=True, stop=False)
                m.matmul(score_bank[n % 3][:, w - P:w], ident_bf[:, :], causal[:, :], start=False, stop=True
                         ).then_inc(score_psum, 1)

            def transpose_prob(n):
                pe.wait_ge(prob_ready, n + 1)
                if n >= 2:
                    pe.wait_ge(probT_ready, n - 1)
                for j in range(n % TB + 1):
                    last = m.transpose(probT_bank[n % 2][:, j * P:(j + 1) * P], prob[:, n % 4, j * P:(j + 1) * P],
                                       ident[:, :])
                last.then_inc(probT_psum, 1)

            def project_values(b, first=0, end=TB):
                if first == 0:
                    if b == 0:
                        pe.wait_ge(zT_ready[0], 1)
                    if b == 1:
                        pe.wait_ge(zT_ready[1], 1)
                    if b == 2:
                        pe.wait_ge(values_ready, 2)
                    if b == 3:
                        pe.wait_ge(order_ready, 1)
                for i in range(first, end):
                    t = b * TB + i
                    last = m.matmul(values_bank[b][:, i * D:(i + 1) * D], xnT[:, t * P:(t + 1) * P], wvT[:, :],
                                    start=True, stop=True)
                if end == TB:
                    last.then_inc(values_psum, 1)

            def weigh_values(n):
                b, q = divmod(n, TB)
                pe.wait_ge(probT_ready, n + 1)
                pe.wait_ge(values_ready, b + 1)
                if q == 0 and b >= 2:
                    pe.wait_ge(attn_ready, b - 1)
                if b == B - 1 and q > 0:
                    pe.wait_ge(masked_ready, NT)
                if b == B - 1:
                    where = last_attn_bank[q][:, 0:D]
                elif (b, q) == (B - 2, TB - 1):
                    where = spare_attn_bank[:, 0:D]
                else:
                    where = attn_bank[b % 2][:, q * D:(q + 1) * D]
                for j in range(q + 1):
                    last = m.matmul(where, probT[:, b % 2, j, q * P:(q + 1) * P], values[:, b * TB + j, :],
                                    start=(j == 0), stop=(j == q))
                last.then_inc(attn_psum, 1)

            def attend(n, first, end):
                if n < end and n < NT - 1:
                    if n == first > 0:
                        pe.wait_ge(rowsT_ready, NT // TB)
                    if n == first + 1 > 1:
                        pe.wait_ge(hidT_ready, PAIRS)
                    scores(n)
                if first <= n - 3 < end:
                    if n - 3 == first > 0:
                        pe.wait_ge(mixed_ready, PAIRS)
                    transpose_prob(n - 3)
                if n == NT - 2:
                    scores(NT - 1)
                if first <= n - 4 < end:
                    weigh_values(n - 4)

            tiles, down_starts = [], []

            def load_pairs(c):
                if c == 0:
                    pe.wait_ge(pairs_ready, 1)
                numbers = load_numbers(pe, pair_numbers, "number", c, 3, [NT - 1, (E - 1) * H2, (E - 1) * H])
                tiles.extend(numbers[0::3])
                down_starts.extend(numbers[2::3])

            def transpose_rows(c):
                if c >= 2:
                    pe.wait_ge(rowsT_ready, c - 1)
                if c == 0:
                    pe.wait_ge(masked_ready, EARLY - 2)
                if c == 1:
                    pe.wait_ge(values_ready, B)
                for i in range(TB):
                    pe.wait_ge(gathered[c * TB + i], 16)
                    last = m.transpose(rowsT_bank[c % 2][:, i * P:(i + 1) * P], rows[:, c * TB + i, 0:D], ident[:, :])
                last.then_inc(rowsT_psum, 1)

            pe.wait_ge(consts_made, 2)
            scores(0)
            scores(1)
            pe.wait_ge(xnT_ready, B)
            scores(2)
            project_values(0, 0, TB // 2)
            rank_tokens()
            attend(3, 0, EARLY)
            project_values(0, TB // 2, TB)
            project_values(1)
            project_queries(2)
            pe.wait_ge(values_ready, 1)
            project_queries(3)
            project_values(2, 0, TB // 2)
            invert_order()
            project_values(2, TB // 2, TB)
            pe.wait_ge(zT_ready[2], 1)
            pe.wait_ge(zT_ready[3], 1)
            for n in range(4, EARLY):
                attend(n, 0, EARLY)
                if n == EARLY - 1:
                    transpose_rows(0)
                    load_pairs(0)
                if n == EARLY - 1:
                    project_values(3)

            def step(n):
                if n in TRANSPOSE:
                    transpose_rows(TRANSPOSE[n])
                t = n
                if exists(t):
                    pe.wait_ge(rowsT_ready, min(t, NT - 1) // TB + 1)
                    pe.wait_ge(up_cur_ready, t + 1)
                    if t >= 2:
                        pe.wait_ge(hidT_ready, t - 1)
                    else:
                        pe.wait_ge(masked_ready, EARLY)
                    for c in range(H2 // P):
                        last = m.matmul(up_bank[t % 2][:, c * P:(c + 1) * P], up_cur[:, t % 3, c * P:(c + 1) * P],
                                        tile_at(rowsT, tiles[t]), start=True, stop=True)
                    last.then_inc(up_psum, 1)
                if n == PAIRS - 1:
                    attend(EARLY, EARLY, NT)
                t = n + 2
                if exists(t) and t % CHUNK == 0 and t > 0:
                    load_pairs(t // CHUNK)
                t = n - 2
                if exists(t):
                    pe.wait_ge(hidT_ready, t + 1)
                    if t < 2:
                        pe.wait_ge(down_loaded, 16)
                        pe.wait_ge(probT_ready, EARLY)
                    else:
                        pe.wait_ge(mixed_ready, t - 1)
                    for c in range(HC):
                        last = m.matmul(down_bank[t % 2][:, 0:D], hidT[:, t % 3, c, :],
                                        down[:, bass.ds(down_starts[t] + c * D, D)], start=(c == 0), stop=(c == HC - 1))
                    last.then_inc(down_psum, 1)
                if n in DRAIN:
                    attend(DRAIN[n], 0, EARLY)

            for n in STEPS:
                step(n)
            for n in range(EARLY + 1, NT + 4):
                attend(n, EARLY, NT)


_INS = ["L0_attn_x", "L0_attn_WQ", "L0_attn_WK", "L0_attn_WV",
        "L0_ffn_scale", "L0_ffn_centroids", "L0_ffn_up_w", "L0_ffn_down_w"]


def kernel(**inputs):
    import numpy as _np
    import concourse.bacc as _bacc
    from concourse import mybir as _mybir
    from concourse.bass_utils import run_bass_kernel_spmd as _run

    nc = _bacc.Bacc("TRN2", target_bir_lowering=False, num_devices=1)
    arrays, args = {}, []
    for name in _INS:
        a = _np.ascontiguousarray(inputs[name])
        arrays[f"in_{name}_dram"] = a
        args.append(nc.dram_tensor(f"in_{name}_dram", a.shape, _mybir.dt.from_np(a.dtype), kind="ExternalInput").ap())
    batch, seq, dim = inputs["L0_attn_x"].shape
    out = nc.dram_tensor("out_0_dram", (batch, seq, dim), _mybir.dt.float32, kind="ExternalOutput").ap()
    xf_dram = nc.dram_tensor("xf_dram", (batch * seq, dim + 1), _mybir.dt.float32).ap()
    gate_dram = nc.dram_tensor("gate_dram", (batch * seq, dim), _mybir.dt.float32).ap()
    build(nc, *args, out, xf_dram, gate_dram)
    r = _run(nc, [arrays], core_ids=[0])
    return r.results[0]["out_0_dram"]
```
